# Optimizing a Trainium2 kernel written in Bass

```python
import numpy as np
import jax
import jax.numpy as jnp

def _softmax(x, axis=-1):
    return jax.nn.softmax(x, axis=axis)

def _gelu(x):
    return jax.nn.gelu(x, approximate=True)

def _silu(x):
    return jax.nn.silu(x)

def _sigmoid(x):
    return jax.nn.sigmoid(x)

def _layernorm(x, axis=-1, eps=1e-05):
    m = jnp.mean(x, axis=axis, keepdims=True)
    v = jnp.var(x, axis=axis, keepdims=True)
    return (x - m) / jnp.sqrt(v + eps)

def _scatter_add(tgt, idx, src, axis=0):
    return tgt.at[idx].add(src)

def _segment_sum(src, seg, n):
    return jax.ops.segment_sum(src, seg, n)
kernel_name = 'mk_xattn_ffn_d1_seqx_r8_0ee34e'

def setup_inputs(seed: int=0):
    np.random.seed(seed)
    _w = jnp.asarray

    def _rec_inputs():
        import jax
        import jax.numpy as jnp
        _rk = jax.random.key(seed)
        x = -0.0002928 + 1 * jax.random.normal(jax.random.fold_in(_rk, 1), (16, 256, 128), jnp.float32)
        _lenS = 256 - jax.random.randint(jax.random.fold_in(_rk, 7), (16,), 0, max(1, 256 // 4) + 1, jnp.int32)
        _lenS2 = 64 - jax.random.randint(jax.random.fold_in(_rk, 8), (16,), 0, max(1, 64 // 4) + 1, jnp.int32)
        _ctx_1024P = jax.random.normal(jax.random.fold_in(_rk, 11), (16, 16, 128), jnp.float32)
        _ctx_1024c = jax.random.dirichlet(jax.random.fold_in(_rk, 511), 0.3 * jnp.ones((16,), jnp.float32), (16, 64))
        _ctx_1024t = jnp.einsum('bsk,bkd->bsd', _ctx_1024c, _ctx_1024P)
        _ctx_1024t = _ctx_1024t * jax.lax.rsqrt(jnp.mean(jnp.square(_ctx_1024t)) + 1e-12) * 0.953939
        ctx_1024 = -1.39393e-06 + 0.999914 * (_ctx_1024t + 0.3 * jax.random.normal(jax.random.fold_in(_rk, 611), (16, 64, 128), jnp.float32))
        _validS = jnp.arange(256)[None, :] < _lenS[:, None]
        _validS2 = jnp.arange(64)[None, :] < _lenS2[:, None]
        _causal = jnp.tril(jnp.ones((256, 256), dtype=bool))
        mask_1x1xSxS2_if1 = jnp.where(jnp.ones((1, 1, 256, 64), dtype=bool), 1, 0).astype(jnp.int32)
        return (x, ctx_1024, mask_1x1xSxS2_if1)
    x, ctx_1024, mask_1x1xSxS2_if1 = _rec_inputs()

    def _L0_xattn_setup():
        import jax, jax.numpy as jnp
        import numpy as np
        import math
        B, S, D, H = (2, 256, 128, 16)
        DK = D // H
        key = jax.random.key(seed)
        ks = jax.random.split(key, 8)
        scale = 0.02
        return {'qi': jax.random.normal(ks[0], (B, S, D), dtype=jnp.float32), 'ki': jax.random.normal(ks[1], (B, S, D), dtype=jnp.float32), 'vi': jax.random.normal(ks[2], (B, S, D), dtype=jnp.float32), 'mask': jnp.ones((1, 1, S, S), dtype=jnp.int32), 'Wq': jax.random.normal(ks[3], (D, D), dtype=jnp.float32) * scale, 'Wk': jax.random.normal(ks[4], (D, D), dtype=jnp.float32) * scale, 'Wv': jax.random.normal(ks[5], (D, D), dtype=jnp.float32) * scale, 'Wo': jax.random.normal(ks[6], (D, D), dtype=jnp.float32) * scale}
    _L0_xattn_all = _L0_xattn_setup()
    _L0_xattn_in = {k: v for k, v in _L0_xattn_all.items() if k in ('Wq', 'Wk', 'Wv', 'Wo')}
    del _L0_xattn_all

    def _L0_ffn_setup():
        import jax, jax.numpy as jnp
        import numpy as np
        D = 128
        F = 4 * D
        E = 8
        NS = 2
        TOP_K = 2
        B, S = (2, 128)
        key = jax.random.key(seed)
        ks = jax.random.split(key, 7)
        w = 1.0 / np.sqrt(D)
        wf = 1.0 / np.sqrt(F)
        return {'x': jax.random.normal(ks[0], (B, S, D), jnp.float32), 'centroids': jax.random.normal(ks[1], (E, D), jnp.float32) * w, 'routing_bias': jnp.zeros((E,), jnp.float32), 'Wfc_r': jax.random.normal(ks[2], (E, F, D), jnp.float32) * w, 'Wproj_r': jax.random.normal(ks[3], (E, D, F), jnp.float32) * wf, 'Wfc_sh': jax.random.normal(ks[4], (NS, F, D), jnp.float32) * w, 'Wproj_sh': jax.random.normal(ks[5], (NS, D, F), jnp.float32) * wf}
    _L0_ffn_all = _L0_ffn_setup()
    _L0_ffn_in = {k: v for k, v in _L0_ffn_all.items() if k in ('centroids', 'routing_bias', 'Wfc_r', 'Wproj_r', 'Wfc_sh', 'Wproj_sh')}
    del _L0_ffn_all
    return {'x': x, 'ctx_1024': ctx_1024, 'mask_1x1xSxS2_if1': mask_1x1xSxS2_if1, 'L0_xattn_Wq': _L0_xattn_in['Wq'], 'L0_xattn_Wk': _L0_xattn_in['Wk'], 'L0_xattn_Wv': _L0_xattn_in['Wv'], 'L0_xattn_Wo': _L0_xattn_in['Wo'], 'L0_ffn_centroids': _L0_ffn_in['centroids'], 'L0_ffn_routing_bias': _L0_ffn_in['routing_bias'], 'L0_ffn_Wfc_r': _L0_ffn_in['Wfc_r'], 'L0_ffn_Wproj_r': _L0_ffn_in['Wproj_r'], 'L0_ffn_Wfc_sh': _L0_ffn_in['Wfc_sh'], 'L0_ffn_Wproj_sh': _L0_ffn_in['Wproj_sh']}

def reference(x, ctx_1024, mask_1x1xSxS2_if1, L0_xattn_Wq, L0_xattn_Wk, L0_xattn_Wv, L0_xattn_Wo, L0_ffn_centroids, L0_ffn_routing_bias, L0_ffn_Wfc_r, L0_ffn_Wproj_r, L0_ffn_Wfc_sh, L0_ffn_Wproj_sh):
    import jax
    import jax.numpy as jnp

    def _L0_xattn_ref(qi, ki, vi, mask, Wq, Wk, Wv, Wo):
        import jax, jax.numpy as jnp
        import numpy as np
        import math
        B, S, D, H = (2, 256, 128, 16)
        DK = D // H
        b, sq, d = qi.shape
        sk = ki.shape[1]
        q = jnp.einsum('bsd,ed->bse', qi, Wq).reshape(b, sq, H, DK).transpose(0, 2, 1, 3)
        k = jnp.einsum('bsd,ed->bse', ki, Wk).reshape(b, sk, H, DK).transpose(0, 2, 1, 3)
        v = jnp.einsum('bsd,ed->bse', vi, Wv).reshape(b, sk, H, DK).transpose(0, 2, 1, 3)
        scores = jnp.einsum('bhqd,bhkd->bhqk', q, k) / math.sqrt(DK)
        attn = jax.nn.softmax(scores, axis=1)
        x = jnp.einsum('bhqk,bhkd->bhqd', attn, v)
        x = x.transpose(0, 2, 1, 3).reshape(b, sq, H * DK)
        out = jnp.einsum('bsd,ed->bse', x, Wo)
        return out

    def _L0_ffn_ref(x, centroids, routing_bias, Wfc_r, Wproj_r, Wfc_sh, Wproj_sh):
        import jax, jax.numpy as jnp
        import numpy as np
        D = 128
        F = 4 * D
        E = 8
        NS = 2
        TOP_K = 2
        B, S = (2, 128)
        raw = jnp.einsum('bsd,ed->bse', x, centroids)
        routing_scores = jax.nn.sigmoid(raw)
        balanced = jax.nn.sigmoid(raw + routing_bias)
        _, top_idx = jax.lax.top_k(balanced, TOP_K)
        gathered = jnp.take_along_axis(routing_scores, top_idx, axis=-1)
        top_w = jax.nn.softmax(gathered, axis=-1)
        combine = jnp.sum(jax.nn.one_hot(top_idx, E, dtype=x.dtype) * top_w[..., None], axis=-2)
        h_sh = jax.nn.gelu(jnp.einsum('bsd,nfd->bsnf', x, Wfc_sh), approximate=False)
        shared_out = jnp.einsum('bsnf,ndf->bsd', h_sh, Wproj_sh)
        h_r = jax.nn.gelu(jnp.einsum('bsd,efd->bsef', x, Wfc_r), approximate=False)
        expert_out = jnp.einsum('bsef,edf->bsed', h_r, Wproj_r)
        routed_out = jnp.einsum('bsed,bse->bsd', expert_out, combine)
        return x + shared_out + routed_out
    x = x + _L0_xattn_ref(_layernorm(x, axis=-1), ctx_1024, ctx_1024, mask_1x1xSxS2_if1, L0_xattn_Wq, L0_xattn_Wk, L0_xattn_Wv, L0_xattn_Wo)
    x = x + _L0_ffn_ref(_layernorm(x, axis=-1), L0_ffn_centroids, L0_ffn_routing_bias, L0_ffn_Wfc_r, L0_ffn_Wproj_r, L0_ffn_Wfc_sh, L0_ffn_Wproj_sh)
    return x

_drawn_inputs = setup_inputs


def setup_inputs(seed=0):
    import zlib

    import numpy as np

    out = dict(_drawn_inputs(seed))
    spreads = {'L0_ffn_routing_bias': (0.0, 0.1)}
    factors = {'L0_xattn_Wq': 5.039, 'L0_xattn_Wk': 4.903}
    for name, (base, spread) in spreads.items():
        noise = np.random.default_rng([zlib.crc32(name.encode()), seed]).standard_normal(out[name].shape)
        drawn = base * np.exp(spread * noise) if base else spread * noise
        out[name] = jnp.asarray(drawn.astype(out[name].dtype))
    for name, factor in factors.items():
        out[name] = (out[name] * factor).astype(out[name].dtype)
    return out
```

```python
import numpy as np
from contextlib import ExitStack

import concourse.bass as bass
from concourse import mybir

F32 = mybir.dt.float32
F16 = mybir.dt.float16
BF16 = mybir.dt.bfloat16
ALU = mybir.AluOpType
ACT = mybir.ActivationFunctionType
AX_X = mybir.AxisListType.X

P = 128
D = 128
B, S, SK = 16, 256, 64
H, DK = 16, 8
HH = H // 2
PAIRS = B // 2
TILES = B * S // P
TP = TILES // PAIRS
UNITS = 2 * PAIRS
EXPERTS, SHARED = 8, 2
NE = EXPERTS + SHARED
F = 4 * D
FC = F // P
EPS = 1e-5
W_SCALE = 64.0
NBANK = 8
BANK = 512


def xattn_moe_kernel(nc, x, ctx_t, wq_t, wk_t, wv_t, wo_t, cent_t, rbias, wfc_t, wproj_t, out):
    with ExitStack() as stack:
        def sb(name, shape, dt=F32):
            return stack.enter_context(nc.sbuf_tensor(name, shape, dt))

        def sem(name):
            return stack.enter_context(nc.semaphore(name))

        X = sb("X", [P, PAIRS, 2, 2, D])
        ctxT = sb("ctxT", [P, PAIRS, 2, SK])
        wq, wk, wv = (sb(n, [P, D]) for n in ("wq", "wk", "wv"))
        wo = sb("wo", [P, 2, 2, D])
        cent = sb("cent", [P, EXPERTS])
        centH = sb("centH", [P, EXPERTS], F16)
        centL = sb("centL", [P, EXPERTS], F16)
        bias8 = sb("bias8", [P, EXPERTS])
        ident = sb("ident", [P, P])
        negI = sb("negI", [P, P], BF16)
        head_mask = sb("head_mask", [P, HH])
        eps = sb("eps", [P, 1])
        kT = sb("kT", [P, 2, PAIRS, SK])
        V = sb("V", [P, PAIRS, D])
        kPad = sb("kPad", [P, 2, 2, HH, 2, SK])
        vPad = [sb(f"vPad{j}", [P, 2, HH * (P + DK)]) for j in range(2)]
        qT = sb("qT", [P, PAIRS, 2, S])
        xn = sb("xn", [P, 2, TP, D])
        xnT = sb("xnT", [P, 2, TP * P])
        stats = sb("stats", [P, 2, TP, 6])
        mv = sb("mv", [P, 2, TP, 2])
        sd = sb("sd", [P, 2, TP])
        rstd = sb("rstd", [P, 2, TP])
        Mx = sb("Mx", [P, 2, P], BF16)
        Z = sb("Z", [P, 2, P])
        rZ = sb("rZ", [P, 2, P])
        E = sb("E", [P, 4, H, P])
        oT = sb("oT", [P, 2, 2, P])
        x2H = sb("x2H", [P, TILES * P], F16)
        x2L = sb("x2L", [P, TILES * P], F16)
        wfcH = sb("wfcH", [P, NE, F], F16)
        wfcL = sb("wfcL", [P, NE, F], F16)
        wproj = sb("wproj", [P, NE, FC, D])
        hid = sb("hid", [P, 2, FC, BANK])
        comb = sb("comb", [P, TILES, NE])
        wfc_f32 = E[:, :, :, :].rearrange("p a h q -> p (a h q)")[:, 0:NE * F].rearrange(
            "p (e f) -> p e f", e=NE)
        NR = 12
        E_flat = E[:, :, :, :].rearrange("p a h q -> p (a h q)")
        rt = E_flat[:, 0:NR * TILES * EXPERTS].rearrange("p (n t e) -> p n t e", n=NR, t=TILES)
        r1 = E_flat[:, NR * TILES * EXPERTS:(NR * EXPERTS + 12) * TILES].rearrange("p (n t) -> p n t", n=12)
        iota8 = sb("iota8", [P, EXPERTS])

        banks = stack.enter_context(nc.psum_tensor("banks", [P, NBANK, BANK], F32))
        k_ps = [banks[:, i, :] for i in (0, 1)]
        v_ps = [banks[:, i, :] for i in (2, 3)]
        t_ps = [banks[:, i, :] for i in (4, 5)]
        q_ps = [banks[:, i, :] for i in (6, 7)]
        scores = banks[:, 0:4, :]
        o_ps = banks[:, 4, :]
        y_ps = banks[:, 5, :]
        t2_ps = [banks[:, i, :] for i in (6, 7)]
        r_ps = [banks[:, i, :] for i in (4, 5)]
        up_ps = [banks[:, i, :] for i in (0, 1, 2, 3)]
        dn_ps = [banks[:, i, :] for i in (4, 5)]

        ctx_loaded, wq_loaded, wo_loaded = sem("ctx_loaded"), sem("wq_loaded"), sem("wo_loaded")
        x_loaded = [sem(f"x_loaded{q}") for q in range(4)]
        wfc_loaded, wproj_loaded, small_loaded = sem("wfc_loaded"), sem("wproj_loaded"), sem("small_loaded")
        masks = sem("masks")
        k_ready, v_ready = sem("k_ready"), sem("v_ready")
        kT_ready, V_ready = sem("kT_ready"), sem("V_ready")
        wfcH_ready, wfcL_ready = sem("wfcH_ready"), sem("wfcL_ready")
        ln_step = sem("ln_step")
        mv_ready, sd_ready = sem("mv_ready"), sem("sd_ready")
        xn_ready, t_ready, xnT_ready, q_ready, qT_ready = (
            sem(n) for n in ("xn_ready", "t_ready", "xnT_ready", "q_ready", "qT_ready"))
        kPad_ready, vPad_ready = sem("kPad_ready"), sem("vPad_ready")
        raw_ready, max_ready, s_ready = sem("raw_ready"), sem("max_ready"), sem("s_ready")
        exp_done, z_ready, rz_ready, attn_ready = (
            sem(n) for n in ("exp_done", "z_ready", "rz_ready", "attn_ready"))
        o_ready, oT_ready, y_ready, x_added = (sem(n) for n in ("o_ready", "oT_ready", "y_ready", "x_added"))
        xn2_ready, x2_added, t2_ready, x2H_ready, x2L_ready = (
            sem(n) for n in ("xn2_ready", "x2_added", "t2_ready", "x2H_ready", "x2L_ready"))
        ln2_step, mv2_ready, sd2_ready = sem("ln2_step"), sem("mv2_ready"), sem("sd2_ready")
        route_ready, raw_copied, rstep, rexp, comb_ready = (
            sem(n) for n in ("route_ready", "raw_copied", "rstep", "rexp", "comb_ready"))
        rneed = sem("rneed")
        up_ready, h_ready, dn_ready, acc_done = (
            sem(n) for n in ("up_ready", "h_ready", "dn_ready", "acc_done"))
        stored = sem("stored")

        block = stack.enter_context(nc.Block())

        @block.sync
        def _(sp):
            sp.dma_start(ctxT[:], ctx_t).then_inc(ctx_loaded, 16)
            sp.dma_start(wk[:], wk_t).then_inc(ctx_loaded, 16)
            sp.dma_start(wv[:], wv_t).then_inc(ctx_loaded, 16)
            xv = x.rearrange("(q t p) d -> q p t d", q=4, p=P)
            Xv = X[:].rearrange("p (q a) b c d -> p q (a b c) d", q=4)
            for q in range(4):
                sp.dma_start(Xv[:, q], xv[q]).then_inc(x_loaded[q], 16)
                if q == 0:
                    sp.dma_start(wq[:], wq_t).then_inc(wq_loaded, 16)
            for b in range(2):
                for half in range(2):
                    sp.dma_start(wo[64 * b:64 * b + 64, b, half, :],
                                 wo_t[64 * half:64 * half + 64, :]).then_inc(wo_loaded, 16)
            sp.dma_start(wfc_f32, wfc_t).then_inc(wfc_loaded, 16)
            sp.dma_start(cent[:], cent_t).then_inc(small_loaded, 16)
            sp.dma_start(bias8[:], rbias).then_inc(small_loaded, 16)
            sp.dma_start(wproj[:], wproj_t).then_inc(wproj_loaded, 16)
            ov = out.rearrange("(a t p) d -> p a t d", a=PAIRS, p=P)
            Xo = X[:].rearrange("p a b c d -> p a (b c) d")
            with sp.Fori(0, PAIRS) as a:
                sp.wait_ge(acc_done, a * NE + NE)
                sp.dma_start(ov[:, a], Xo[:, a]).then_inc(stored, 16)
            sp.wait_ge(stored, 16 * PAIRS)

        @block.gpsimd
        def _(pool):
            g = nc.gpsimd
            built = [0]

            def then(ins):
                built[0] += 1
                ins.then_inc(masks, 1)
                pool.wait_ge(masks, built[0])

            then(g.memset(ident[:], 0.0))
            then(g.affine_select(out=ident[:], in_=ident[:], compare_op=ALU.not_equal, fill=1.0, base=0,
                                 pattern=[[-1, P]], channel_multiplier=1))
            then(g.memset(negI[:], 0.0))
            then(g.affine_select(out=negI[:], in_=negI[:], compare_op=ALU.not_equal, fill=-1.0, base=0,
                                 pattern=[[-1, P]], channel_multiplier=1))
            then(g.memset(eps[:], EPS))
            then(g.memset(kPad[:, 0], 0.0))
            then(g.memset(kPad[:, 1], 0.0))
            then(g.memset(vPad[0][:], 0.0))
            then(g.memset(vPad[1][:], 0.0))
            then(g.iota(iota8[:], [[-1, EXPERTS]], base=EXPERTS, channel_multiplier=0,
                        allow_small_or_imprecise_dtypes=True))
            then(g.memset(comb[:, :, 0:SHARED], 1.0))
            then(g.memset(head_mask[:], 1.0))
            for lo in (0, 64):
                m = head_mask[lo:lo + 64, :]
                then(g.affine_select(out=m, in_=m, compare_op=ALU.is_ge, fill=0.0, base=0,
                                     pattern=[[-DK, HH]], channel_multiplier=1))
                then(g.affine_select(out=m, in_=m, compare_op=ALU.is_ge, fill=0.0, base=DK - 1,
                                     pattern=[[DK, HH]], channel_multiplier=-1))
            then(g.memset(wo[64:128, 0, :, :], 0.0))
            then(g.memset(wo[0:64, 1, :, :], 0.0))

            def normalise(k, u):
                pool.wait_ge(rz_ready, u + 1)
                g.tensor_tensor(E[:, k], E[:, k], rZ[:, k % 2, :].unsqueeze(1).broadcast_to([P, H, P]),
                                ALU.mult).then_inc(attn_ready, 1)

            for k in range(4):
                normalise(k, k)
            with pool.Fori(1, UNITS // 4) as n:
                for k in range(4):
                    normalise(k, 4 * n + k)
            with pool.Fori(0, PAIRS // 2) as n:
                for j in range(2):
                    pool.wait_ge(xn2_ready, 2 * n + j + 1)
                    xv = X[:, 2 * n + j].rearrange("p b c d -> p (b c) d")
                    g.tensor_tensor(xv, xv, xn[:, j], ALU.add).then_inc(x2_added, 1)

        @block.scalar
        def _(act):
            s = nc.scalar
            for half in range(2):
                act.wait_ge(k_ready, half + 1)
                s.activation(kT[:, half], k_ps[half], ACT.Copy).then_inc(kT_ready, 1)
            for i in range(2):
                act.wait_ge(v_ready, i + 1)
                s.activation(V[:, 4 * i:4 * i + 4], v_ps[i], ACT.Copy).then_inc(V_ready, 1)
            act.wait_ge(masks, 18)
            def q_side(a, nq):
                act.wait_ge(mv_ready, nq)
                s.activation(sd[:], mv[:, :, :, 1], ACT.Sqrt, bias=eps[:]).then_inc(sd_ready, 1)
                for j in range(2):
                    act.wait_ge(t_ready, a + j + 1)
                    s.activation(xnT[:, j], t_ps[j], ACT.Copy).then_inc(xnT_ready, 1)
                for j in range(2):
                    act.wait_ge(q_ready, a + j + 1)
                    s.activation(qT[:, a + j], q_ps[j], ACT.Copy).then_inc(qT_ready, 1)

            with act.Fori(0, PAIRS // 2) as n:
                q_side(2 * n, n + 1)
            act.wait_ge(wfc_loaded, 16)
            with act.Fori(0, NE) as e:
                s.activation(wfcH[:, e], wfc_f32[:, e], ACT.Copy, scale=W_SCALE).then_inc(wfcH_ready, 1)

            def copy_o(u, k):
                act.wait_ge(o_ready, u + 1)
                s.activation(oT[:, k % 2], o_ps[:, 0:2 * P], ACT.Copy).then_inc(oT_ready, 1)

            def exps(u, k, again):
                act.wait_ge(s_ready, u + 1)
                if again:
                    act.wait_ge(o_ready, u - 3)
                for i in range(2):
                    s.activation(E[:, k, 8 * i:8 * i + 8], scores[:, 2 * i:2 * i + 2], ACT.Exp,
                                 scale=DK ** -0.5).then_inc(exp_done, 1)

            act.wait_ge(wfcL_ready, NE)
            for k in range(4):
                if k >= 2:
                    copy_o(k - 2, k)
                exps(k, k, False)
            with act.Fori(1, UNITS // 4) as n:
                for k in range(4):
                    u = 4 * n
                    act.wait_ge(y_ready, u + k - 3)
                    copy_o(u + k - 2, k)
                    exps(u + k, k, True)
            for k in range(2):
                act.wait_ge(y_ready, UNITS + k - 3)
                copy_o(UNITS - 2 + k, k)

            with act.Fori(0, PAIRS // 2) as n:
                act.wait_ge(mv2_ready, n + 1)
                s.activation(sd[:], mv[:, :, :, 1], ACT.Sqrt, bias=eps[:]).then_inc(sd2_ready, 1)
                for j in range(2):
                    act.wait_ge(t2_ready, 2 * n + j + 1)
                    s.activation(x2H[:, bass.ds((2 * n + j) * BANK, BANK)], t2_ps[j], ACT.Copy).then_inc(x2H_ready, 1)
            act.wait_ge(rneed, 2)
            s.activation(rt[:, 1:3], rt[:, 1:3], ACT.Exp, scale=-1.0).then_inc(rexp, 1)
            act.wait_ge(rneed, 4)
            s.activation(r1[:, 4:6], r1[:, 4:6], ACT.Exp).then_inc(rexp, 1)

            def gelus(i, j, again):
                if again:
                    act.wait_ge(dn_ready, i - 1)
                for c in range(FC):
                    act.wait_ge(up_ready, i * FC + c + 1)
                    s.activation(hid[:, j, c], up_ps[c], ACT.Gelu, scale=1.0 / W_SCALE).then_inc(h_ready, 1)

            for j in range(2):
                gelus(j, j, False)
            with act.Fori(1, PAIRS * NE // 2) as n:
                for j in range(2):
                    gelus(2 * n + j, j, True)

        @block.vector
        def _(dve):
            v = nc.vector

            def pad_k(j, pair):
                for b in range(2):
                    r = slice(64 * b, 64 * b + 64)
                    v.tensor_tensor(kPad[r, j, :, :, b, :],
                                    kT[r, :, pair, :].unsqueeze(2).broadcast_to([64, 2, HH, SK]),
                                    head_mask[r, :].unsqueeze(1).unsqueeze(3).broadcast_to([64, 2, HH, SK]),
                                    ALU.mult).then_inc(kPad_ready, 1)

            def spread_v(j, pair):
                for b in range(2):
                    r = slice(64 * b, 64 * b + 64)
                    dst = vPad[j][r].rearrange("p a (h s) -> p a h s", s=P + DK)[:, :, :, 64 * b:64 * b + DK]
                    src = V[r, pair, :].rearrange("p (a h d) -> p a h d", a=2, d=DK)
                    v.tensor_copy(dst, src).then_inc(vPad_ready, 1)

            def norm_stats(n0, pair0, step, ready):
                for j in range(2):
                    for t in range(TP):
                        v.bn_stats(stats[:, j, t, :], X[:, pair0 + j, t // 2, t % 2, :]).then_inc(step, 1)
                dve.wait_ge(step, n0 + 8)
                for j in range(2):
                    for t in range(TP):
                        last = v.bn_aggr(mv[:, j, t, :], stats[:, j, t, :])
                last.then_inc(ready, 1)

            def norm_apply(n0, pair0, step, xready):
                v.reciprocal(rstd[:], sd[:]).then_inc(step, 1)
                dve.wait_ge(step, n0 + 9)
                for j in range(2):
                    for t in range(TP):
                        last = v.tensor_scalar(xn[:, j, t, :], X[:, pair0 + j, t // 2, t % 2, :],
                                               mv[:, j, t, 0:1], rstd[:, j, t:t + 1], ALU.subtract, ALU.mult)
                    last.then_inc(xready, 1)

            dve.wait_ge(masks, 18)
            dve.wait_ge(kT_ready, 2)
            pad_k(0, 0)
            pad_k(1, 1)
            dve.wait_ge(V_ready, 2)
            spread_v(0, 0)
            spread_v(1, 1)

            def ln1(n, again):
                dve.wait_ge(x_loaded[n], 16)
                norm_stats(9 * n, 2 * n, ln_step, mv_ready)
                dve.wait_ge(sd_ready, n + 1)
                if again:
                    dve.wait_ge(t_ready, 2 * n)
                norm_apply(9 * n, 2 * n, ln_step, xn_ready)

            for n in range(PAIRS // 2):
                ln1(n, n > 0)
            with dve.Fori(0, NE) as e:
                dve.wait_ge(wfcH_ready, e + 1)
                v.scalar_tensor_tensor(wfcL[:, e], wfc_f32[:, e], W_SCALE, wfcH[:, e],
                                       ALU.mult, ALU.subtract).then_inc(wfcL_ready, 1)

            def max_heads(u, k):
                dve.wait_ge(raw_ready, u + 1)
                v.tensor_reduce(Mx[:, k % 2, :], scores.rearrange("p b (h q) -> p q (b h)", q=P),
                                AX_X, ALU.max).then_inc(max_ready, 1)

            def sum_heads(u, k):
                dve.wait_ge(exp_done, 2 * u + 2)
                v.tensor_reduce(Z[:, k % 2, :], E[:, k].rearrange("p h q -> p q h"), AX_X,
                                ALU.add).then_inc(z_ready, 1)
                dve.wait_ge(z_ready, u + 1)
                v.reciprocal(rZ[:, k % 2, :], Z[:, k % 2, :]).then_inc(rz_ready, 1)

            def add_attention(u, qh, pair):
                dve.wait_ge(y_ready, u + 1)
                v.tensor_tensor(X[:, pair, :, qh, :], X[:, pair, :, qh, :],
                                y_ps[:, 0:2 * D].rearrange("p (b d) -> p b d", b=2), ALU.add).then_inc(x_added, 1)

            def four_units(u, pair, first, last):
                for k in range(4):
                    if not (first and k == 0):
                        if not (first and k < 3):
                            dve.wait_ge(attn_ready, u + k - 2)
                        sum_heads(u + k - 1, (k - 1) % 4)
                    if not (first and k < 3):
                        kk = k - 3
                        add_attention(u + kk, kk % 2, pair + (kk // 2))
                        if kk % 2 == 1:
                            spread_v((kk // 2) % 2, pair + kk // 2 + 2)
                    max_heads(u + k, k)
                    if k % 2 == 1 and not last:
                        pad_k(k // 2, pair + k // 2 + 2)

            four_units(0, 0, True, False)
            with dve.Fori(1, PAIRS // 2 - 1) as n:
                four_units(4 * n, 2 * n, False, False)
            four_units(UNITS - 4, PAIRS - 2, False, True)
            dve.wait_ge(attn_ready, UNITS - 2)
            sum_heads(UNITS - 1, 3)
            for k in (1, 2, 3):
                add_attention(UNITS - 4 + k, k % 2, PAIRS - 2 + k // 2)
            dve.wait_ge(x_added, UNITS)

            dve.wait_ge(small_loaded, 32)
            v.tensor_copy(centH[:], cent[:]).then_inc(rstep, 1)
            dve.wait_ge(rstep, 1)
            v.tensor_tensor(centL[:], cent[:], centH[:], ALU.subtract).then_inc(rstep, 1)

            def ln2(n, again):
                norm_stats(9 * n, 2 * n, ln2_step, mv2_ready)
                dve.wait_ge(sd2_ready, n + 1)
                if again:
                    dve.wait_ge(t2_ready, 2 * n)
                    dve.wait_ge(x2_added, 2 * n)
                norm_apply(9 * n, 2 * n, ln2_step, xn2_ready)
                for j in range(2):
                    dve.wait_ge(x2H_ready, 2 * n + j + 1)
                    v.tensor_tensor(x2L[:, bass.ds((2 * n + j) * BANK, BANK)], t2_ps[j],
                                    x2H[:, bass.ds((2 * n + j) * BANK, BANK)], ALU.subtract).then_inc(x2L_ready, 1)
                for j in range(2):
                    dve.wait_ge(route_ready, 2 * n + j + 1)
                    v.tensor_copy(rt[:, 0, bass.ds((2 * n + j) * TP, TP), :],
                                  r_ps[j][:, 0:TP * EXPERTS].rearrange("p (t e) -> p t e", e=EXPERTS)
                                  ).then_inc(raw_copied, 1)

            for n in range(PAIRS // 2):
                ln2(n, n > 0)

            steps = [2]

            def then(ins):
                steps[0] += 1
                ins.then_inc(rstep, 1)
                dve.wait_ge(rstep, steps[0])

            def all8(t):
                return t.unsqueeze(2).broadcast_to([P, TILES, EXPERTS])

            tok8 = [P, TILES, EXPERTS]
            iota_b = iota8[:].unsqueeze(1).broadcast_to(tok8)
            dve.wait_ge(raw_copied, PAIRS)
            v.tensor_copy(rt[:, 1], rt[:, 0]).then_inc(rneed, 1)
            v.tensor_tensor(rt[:, 2], rt[:, 0], bias8[:].unsqueeze(1).broadcast_to(tok8), ALU.add).then_inc(rneed, 1)
            dve.wait_ge(rexp, 1)
            then(v.tensor_scalar(rt[:, 1:3], rt[:, 1:3], 1.0, None, ALU.add))
            then(v.reciprocal(rt[:, 3:5], rt[:, 1:3]))
            sig, bal = rt[:, 3], rt[:, 4]

            def pick(scores_, slot, k):
                then(v.tensor_reduce(r1[:, k], scores_, AX_X, ALU.max))
                then(v.tensor_tensor(rt[:, slot], scores_, all8(r1[:, k]), ALU.is_equal))
                then(v.tensor_tensor(rt[:, slot], rt[:, slot], iota_b, ALU.mult))
                then(v.tensor_reduce(r1[:, k + 1], rt[:, slot], AX_X, ALU.max))
                then(v.tensor_tensor(rt[:, slot + 1], rt[:, slot], all8(r1[:, k + 1]), ALU.is_equal))

            pick(bal, 5, 0)
            then(v.scalar_tensor_tensor(rt[:, 7], rt[:, 6], -4.0, bal, ALU.mult, ALU.add))
            pick(rt[:, 7], 8, 2)
            for n, hot in enumerate((6, 9)):
                then(v.tensor_tensor(rt[:, 10 + n], rt[:, hot], sig, ALU.mult))
                then(v.tensor_reduce(r1[:, 4 + n], rt[:, 10 + n], AX_X, ALU.add))
            then(v.tensor_tensor(r1[:, 6], r1[:, 4], r1[:, 5], ALU.max))
            v.tensor_tensor(r1[:, 4], r1[:, 4], r1[:, 6], ALU.subtract).then_inc(rneed, 1)
            v.tensor_tensor(r1[:, 5], r1[:, 5], r1[:, 6], ALU.subtract).then_inc(rneed, 1)
            dve.wait_ge(rexp, 2)
            then(v.tensor_tensor(r1[:, 7], r1[:, 4], r1[:, 5], ALU.add))
            then(v.reciprocal(r1[:, 8], r1[:, 7]))
            for n in range(2):
                then(v.tensor_tensor(r1[:, 9 + n], r1[:, 4 + n], r1[:, 8], ALU.mult))
            for n, hot in enumerate((6, 9)):
                then(v.tensor_tensor(rt[:, 10 + n], rt[:, hot], all8(r1[:, 9 + n]), ALU.mult))
            v.tensor_tensor(comb[:, :, SHARED:NE], rt[:, 10], rt[:, 11], ALU.add).then_inc(comb_ready, 1)

            dve.wait_ge(comb_ready, 1)
            dve.wait_ge(x2_added, PAIRS)
            def add_expert(pair, e, j, i, again):
                dve.wait_ge(dn_ready, i + 1)
                if again:
                    dve.wait_ge(acc_done, i)
                for t in range(TP):
                    last = v.scalar_tensor_tensor(X[:, pair, t // 2, t % 2, :], dn_ps[j][:, t * D:(t + 1) * D],
                                                  comb[:, pair * TP + t, bass.ds(e, 1)], X[:, pair, t // 2, t % 2, :],
                                                  ALU.mult, ALU.add)
                last.then_inc(acc_done, 1)

            add_expert(0, 0, 0, 0, False)
            add_expert(0, 1, 1, 1, True)
            with dve.Fori(1, NE // 2) as m:
                for j in range(2):
                    add_expert(0, 2 * m + j, j, 2 * m + j, True)
            with dve.Fori(1, PAIRS) as a:
                with dve.Fori(0, NE // 2) as m:
                    for j in range(2):
                        add_expert(a, 2 * m + j, j, a * NE + 2 * m + j, True)

        @block.tensor
        def _(pe):
            t = nc.tensor
            pe.wait_ge(ctx_loaded, 48)
            for half in range(2):
                for b in range(2):
                    last = t.matmul(k_ps[half][64 * b:64 * b + 64, :], wk[:, 64 * half:64 * half + 64],
                                    ctxT[:, :, b], start=True, stop=True)
                last.then_inc(k_ready, 1)
            for i in range(2):
                for p in range(4):
                    last = t.matmul(v_ps[i][:, D * p:D * p + D], ctxT[:, 4 * i + p].rearrange("p b s -> p (b s)"), wv[:],
                                    start=True, stop=True)
                last.then_inc(v_ready, 1)

            pe.wait_ge(masks, 18)
            pe.wait_ge(wq_loaded, 16)

            def q_side(pair, again):
                for j in range(2):
                    pe.wait_ge(xn_ready, pair + j + 1)
                    if again:
                        pe.wait_ge(xnT_ready, pair + j - 1)
                    for i in range(TP):
                        last = t.transpose(t_ps[j][:, P * i:P * i + P], xn[:, j, i, :], ident[:])
                    last.then_inc(t_ready, 1)
                for j in range(2):
                    pe.wait_ge(xnT_ready, pair + j + 1)
                    if again:
                        pe.wait_ge(qT_ready, pair + j - 1)
                    for half in range(2):
                        for b in range(2):
                            last = t.matmul(q_ps[j][64 * b:64 * b + 64, S * half:S * half + S],
                                            wq[:, 64 * half:64 * half + 64], xnT[:, j, S * b:S * b + S],
                                            start=True, stop=True)
                    last.then_inc(q_ready, 1)

            q_side(0, False)
            with pe.Fori(1, PAIRS // 2) as n:
                q_side(2 * n, True)

            def raw_scores(u, k, pair, first):
                for i in range(4):
                    if not first and i % 2 == 0:
                        pe.wait_ge(exp_done, 2 * u + i // 2 - 1)
                    for h in range(4 * i, 4 * i + 4):
                        last = t.matmul(scores[:, i, P * (h % 4):P * (h % 4) + P],
                                        kPad[:, (k // 2) % 2, h // HH, h % HH].rearrange("p b s -> p (b s)"),
                                        qT[:, pair, h // HH, P * (k % 2):P * (k % 2) + P],
                                        start=(h % 4 == 0), stop=False, skip_group_check=True)
                last.then_inc(raw_ready, 1)

            def minus_max(u, k):
                pe.wait_ge(max_ready, u + 1)
                for i in range(4):
                    last = t.matmul(scores[:, i, :], negI[:], Mx[:, k % 2, :].unsqueeze(1).broadcast_to([P, 4, P]),
                                    start=False, stop=True, skip_group_check=True)
                last.then_inc(s_ready, 1)

            def weighted_values(u, k, first):
                pe.wait_ge(attn_ready, u + 1)
                if not first:
                    pe.wait_ge(oT_ready, u)
                for half in range(2):
                    for h in range(HH):
                        last = t.matmul(o_ps[:, P * half:P * half + P],
                                        vPad[k // 2][:, half, h * P:(h + 1) * P],
                                        E[:, k, half * HH + h, :], start=(h == 0), stop=(h == HH - 1))
                last.then_inc(o_ready, 1)

            def project_out(u, k, first):
                pe.wait_ge(oT_ready, u + 1)
                if not first:
                    pe.wait_ge(x_added, u)
                for b in range(2):
                    for half in range(2):
                        last = t.matmul(y_ps[:, D * b:D * b + D], oT[:, k % 2, half], wo[:, b, half],
                                        start=(half == 0), stop=(half == 1))
                last.then_inc(y_ready, 1)

            pe.wait_ge(wo_loaded, 64)
            pe.wait_ge(V_ready, 2)
            pe.wait_ge(kT_ready, 2)

            def four_units(u, pair, first):
                for k in range(4):
                    if not (first and k >= 2):
                        pass
                    if k % 2 == 0:
                        pe.wait_ge(kPad_ready, 2 * pair + k + 2)
                    raw_scores(u + k, k, pair + k // 2, first and k == 0)
                    if not (first and k < 2):
                        if k % 2 == 0:
                            pe.wait_ge(vPad_ready, u + k)
                        weighted_values(u + k - 2, (k - 2) % 4, first and k == 2)
                    minus_max(u + k, k)
                    if not (first and k < 2):
                        project_out(u + k - 2, (k - 2) % 4, first and k == 2)

            four_units(0, 0, True)
            with pe.Fori(1, PAIRS // 2) as n:
                four_units(4 * n, 2 * n, False)
            pe.wait_ge(vPad_ready, 2 * PAIRS)
            for k in (2, 3):
                weighted_values(UNITS - 4 + k, k, False)
                project_out(UNITS - 4 + k, k, False)

            pe.wait_ge(rstep, 2)

            def ffn_side(pair, again):
                for j in range(2):
                    pe.wait_ge(xn2_ready, pair + j + 1)
                    if again:
                        pe.wait_ge(x2L_ready, pair + j - 1)
                    for i in range(TP):
                        last = t.transpose(t2_ps[j][:, P * i:P * i + P], xn[:, j, i, :], ident[:])
                    last.then_inc(t2_ready, 1)
                for j in range(2):
                    pe.wait_ge(x2L_ready, pair + j + 1)
                    pe.wait_ge(x2H_ready, pair + j + 1)
                    if again:
                        pe.wait_ge(raw_copied, pair + j - 1)
                    for i in range(TP):
                        tok = bass.ds((pair + j) * BANK + P * i, P)
                        o = r_ps[j][:, EXPERTS * i:EXPERTS * i + EXPERTS]
                        t.matmul(o, x2H[:, tok], centL[:], start=True, stop=False)
                        t.matmul(o, x2L[:, tok], centH[:], start=False, stop=False)
                        last = t.matmul(o, x2H[:, tok], centH[:], start=False, stop=True)
                    last.then_inc(route_ready, 1)

            ffn_side(0, False)
            with pe.Fori(1, PAIRS // 2) as n:
                ffn_side(2 * n, True)

            pe.wait_ge(wproj_loaded, 16)
            pe.wait_ge(wfcL_ready, NE)

            def expert(pair, e, i, j, again):
                def up(c):
                    if again or j:
                        pe.wait_ge(h_ready, i * FC + c - 3)
                    f = bass.ds(c * P, P)
                    tok = bass.ds(pair * BANK, BANK)
                    t.matmul(up_ps[c], wfcH[:, e, f], x2L[:, tok], start=True, stop=False)
                    t.matmul(up_ps[c], wfcL[:, e, f], x2H[:, tok], start=False, stop=False)
                    t.matmul(up_ps[c], wfcH[:, e, f], x2H[:, tok], start=False, stop=True).then_inc(up_ready, 1)

                def down(c):
                    pe.wait_ge(h_ready, i * FC + c + 1)
                    if c == 0 and again:
                        pe.wait_ge(acc_done, i - 1)
                    for q in range(TP):
                        last = t.matmul(dn_ps[j][:, P * q:P * q + P], hid[:, j, c, P * q:P * q + P],
                                        wproj[:, e, c], start=(c == 0 and q == 0), stop=(c == FC - 1),
                                        skip_group_check=True)
                    return last

                up(0), up(1), up(2)
                down(0)
                up(3)
                down(1), down(2)
                down(3).then_inc(dn_ready, 1)

            expert(0, 0, 0, 0, False)
            expert(0, 1, 1, 1, False)
            with pe.Fori(1, NE // 2) as m:
                for j in range(2):
                    expert(0, 2 * m + j, 2 * m + j, j, True)
            with pe.Fori(1, PAIRS) as a:
                with pe.Fori(0, NE // 2) as m:
                    for j in range(2):
                        expert(a, 2 * m + j, a * NE + 2 * m + j, j, True)


def kernel(**inputs):
    import concourse.bacc as bacc
    from concourse.bass_utils import run_bass_kernel_spmd

    f32 = {k: np.asarray(v) for k, v in inputs.items()}
    arrays = {
        "x": f32["x"].reshape(B * S, D),
        "ctx_t": f32["ctx_1024"].reshape(PAIRS, 2, SK, D).transpose(3, 0, 1, 2),
        "wq_t": f32["L0_xattn_Wq"].T,
        "wk_t": f32["L0_xattn_Wk"].T,
        "wv_t": f32["L0_xattn_Wv"].T,
        "wo_t": f32["L0_xattn_Wo"].T,
        "cent_t": f32["L0_ffn_centroids"].T,
        "rbias": np.broadcast_to(f32["L0_ffn_routing_bias"], (P, EXPERTS)),
        "wfc_t": np.concatenate([f32["L0_ffn_Wfc_sh"], f32["L0_ffn_Wfc_r"]]).transpose(2, 0, 1),
        "wproj_t": np.concatenate([f32["L0_ffn_Wproj_sh"], f32["L0_ffn_Wproj_r"]])
                     .reshape(NE, D, FC, P).transpose(3, 0, 2, 1),
    }
    nc = bacc.Bacc("TRN2", target_bir_lowering=False, num_devices=1)
    arrays = {f"in_{k}": np.ascontiguousarray(a) for k, a in arrays.items()}
    aps = [nc.dram_tensor(k, a.shape, mybir.dt.from_np(a.dtype), kind="ExternalInput").ap()
           for k, a in arrays.items()]
    out = nc.dram_tensor("out", (B * S, D), F32, kind="ExternalOutput").ap()
    xattn_moe_kernel(nc, *aps, out)
    r = run_bass_kernel_spmd(nc, [arrays], core_ids=[0])
    return r.results[0]["out"].reshape(B, S, D)
```

```python
import numpy as np
from contextlib import ExitStack

import concourse.bass as bass
from concourse import mybir

F32 = mybir.dt.float32
F16 = mybir.dt.float16
I32 = mybir.dt.int32
BF16 = mybir.dt.bfloat16
ALU = mybir.AluOpType
ACT = mybir.ActivationFunctionType
AX_X = mybir.AxisListType.X

P = 128
D = 128
B, S, SK = 16, 256, 64
H, DK = 16, 8
HH = H // 2
PAIRS = B // 2
TILES = B * S // P
TP = TILES // PAIRS
UNITS = 2 * PAIRS
EXPERTS, SHARED = 8, 2
NE = EXPERTS + SHARED
F = 4 * D
FC = F // P
EPS = 1e-5
W_SCALE = 64.0
REGION = B * S + 2 * P
GT = 2 * P
MAX_TILES = 2 * B * S // GT + EXPERTS
ROW = 2 * D + 2
NG = 8
BASICS, BUILT = 11, 27
SKIP = 1 << 20
NBANK = 8
BANK = 512


def xattn_moe_kernel(nc, x, ctx_t, wq_t, wk_t, wv_t, wo_t, cent_t, rbias, wfc_t, wproj_t, out, gathered, results):
    with ExitStack() as stack:
        def sb(name, shape, dt=F32):
            return stack.enter_context(nc.sbuf_tensor(name, shape, dt))

        def sem(name):
            return stack.enter_context(nc.semaphore(name))

        X = sb("X", [P, PAIRS, 2, 2, D])
        ctxT = sb("ctxT", [P, PAIRS, 2, SK])
        wq, wk, wv = (sb(n, [P, D]) for n in ("wq", "wk", "wv"))
        wo = sb("wo", [P, 2, 2, D])
        cent = sb("cent", [P, EXPERTS])
        centH = sb("centH", [P, EXPERTS], F16)
        centL = sb("centL", [P, EXPERTS], F16)
        bias8 = sb("bias8", [P, EXPERTS])
        ident = sb("ident", [P, P])
        negI = sb("negI", [P, P], BF16)
        head_mask = sb("head_mask", [P, HH])
        eps = sb("eps", [P, 1])
        kT = sb("kT", [P, 2, PAIRS, SK])
        V = sb("V", [P, PAIRS, D])
        kPad = sb("kPad", [P, 2, 2, HH, 2, SK])
        vPad = [sb(f"vPad{j}", [P, 2, HH * (P + DK)]) for j in range(2)]
        qT = sb("qT", [P, PAIRS, 2, S])
        xn = sb("xn", [P, 2, TP, D])
        xnT = sb("xnT", [P, 2, TP * P])
        mv = sb("mv", [P, TILES, 2])
        sd = sb("sd", [P, TILES])
        rstd = sb("rstd", [P, TILES])
        shift = sb("shift", [P, TILES])
        stats = sb("stats", [P, 2 * TP, 6])
        mv2 = sb("mv2", [P, 2 * TP, 2])
        var2 = sb("var2", [P, 2 * TP])
        newton = sb("newton", [P, 2 * TP])
        rstd2 = sb("rstd2", [P, 2 * TP])
        shift2 = sb("shift2", [P, 2 * TP])
        consts = sb("consts", [P, 3, 2 * TP])
        xs = sb("xs", [P, TILES, ROW], F16)
        Mx = sb("Mx", [P, 2, P], BF16)
        Z = sb("Z", [P, 2, P])
        rZ = sb("rZ", [P, 2, P])
        E = sb("E", [P, 4, H, P])
        oT = sb("oT", [P, 2, 2, P])
        x2 = sb("x2", [P, 2, TILES * P], F16)
        wfcH = sb("wfcH", [P, NE, F], F16)
        wfcL = sb("wfcL", [P, NE, F], F16)
        wproj = sb("wproj", [P, NE, FC, D])
        gate = sb("gate", [P, 2, TILES])
        ident16 = sb("ident16", [P, P], F16)
        before = sb("before", [P, P], BF16)
        ones16 = sb("ones16", [P, P], BF16)
        member = sb("member", [P, EXPERTS, TILES], BF16)
        newrow = sb("newrow", [P, EXPERTS, TILES])
        region = sb("region", [P, EXPERTS, TILES])
        tile_no = sb("tile_no", [P, MAX_TILES, EXPERTS])
        slot = sb("slot", [P, 2, TILES], I32)
        token = sb("token", [P, 2, TILES], I32)
        counts = sb("counts", [P, EXPERTS], I32)
        tiles_of = sb("tiles_of", [P, EXPERTS], I32)
        table = sb("table", [P, 2, MAX_TILES], I32)
        padding = sb("padding", [P, 2, ROW], F16)
        kPad_flat = kPad[:].rearrange("p j a h b s -> p (j a h b s)")
        xg = kPad_flat[:, 0:NG * ROW].bitcast(F16).rearrange("p (k s r) -> p k s r", k=NG, s=2)
        xgT = kPad_flat[:, 3072:3072 + 2 * GT].bitcast(F16).rearrange("p (k l q) -> p k l q", k=2, l=2)
        yg = vPad[0][:].rearrange("p a s -> p (a s)")[:, 0:NG * 2 * D].rearrange("p (k s d) -> p k s d", k=NG, s=2)
        wfc_f32 = E[:, :, :, :].rearrange("p a h q -> p (a h q)")[:, 0:NE * F].rearrange(
            "p (e f) -> p e f", e=NE)
        NR = 12
        E_flat = E[:, :, :, :].rearrange("p a h q -> p (a h q)")
        rt = E_flat[:, 0:NR * TILES * EXPERTS].rearrange("p (n t e) -> p n t e", n=NR, t=TILES)
        r1 = E_flat[:, NR * TILES * EXPERTS:(NR * EXPERTS + 12) * TILES].rearrange("p (n t) -> p n t", n=12)
        hid = E_flat[:, 4096:8192].rearrange("p (j c q) -> p j c q", j=2, c=FC)
        stats1 = E_flat[:, NE * F:NE * F + TILES * 6].rearrange("p (t s) -> p t s", s=6)
        yk = qT[:].rearrange("p a b q -> p (a b q)").rearrange("p (j k t d) -> p j k t d", j=4, k=2, t=TP)
        hid_g = hid.rearrange("p j c q -> p j (c q)")[:, :, 0:FC * GT].rearrange("p j (c q) -> p j c q", c=FC)
        iota8 = sb("iota8", [P, EXPERTS])

        banks = stack.enter_context(nc.psum_tensor("banks", [P, NBANK, BANK], F32))
        k_ps = [banks[:, i, :] for i in (0, 1)]
        v_ps = [banks[:, i, :] for i in (2, 3)]
        t_ps = [banks[:, i, :] for i in (4, 5)]
        q_ps = [banks[:, i, :] for i in (6, 7)]
        scores = banks[:, 0:4, :]
        o_ps = banks[:, 4, :]
        y_ps = banks[:, 5, :]
        t2_ps = [banks[:, 2 * i:2 * i + 2, :] for i in (0, 1)]
        r_ps = [banks[:, i, :] for i in (6, 7)]
        rank_ps, tot_ps = (banks[:, 6, i * 256:i * 256 + 256].rearrange("p (e t) -> p e t", e=EXPERTS)
                           for i in (0, 1))
        up_ps = [banks[:, i, :] for i in (0, 1, 2, 3)]
        dn_ps = [banks[:, i, :] for i in (4, 5)]
        g_ps = [banks[:, i, 0:BANK // 2].bitcast(F16).rearrange("p (l q) -> p l q", l=2) for i in (6, 7)]

        ctx_loaded, wq_loaded, wo_loaded = sem("ctx_loaded"), sem("wq_loaded"), sem("wo_loaded")
        x_loaded = [sem(f"x_loaded{q}") for q in range(4)]
        wfc_loaded, wproj_loaded, small_loaded = sem("wfc_loaded"), sem("wproj_loaded"), sem("small_loaded")
        masks = sem("masks")
        k_ready, v_ready = sem("k_ready"), sem("v_ready")
        kT_ready, V_ready = sem("kT_ready"), sem("V_ready")
        wfcH_ready, wfcL_ready = sem("wfcH_ready"), sem("wfcL_ready")
        ln_step = sem("ln_step")
        mv_ready, sd_ready, rstd_ready = sem("mv_ready"), sem("sd_ready"), sem("rstd_ready")
        xn_ready, xn1_ready, t_ready, xnT_ready, q_ready, qT_ready = (
            sem(n) for n in ("xn_ready", "xn1_ready", "t_ready", "xnT_ready", "q_ready", "qT_ready"))
        kPad_ready, vPad_ready = sem("kPad_ready"), sem("vPad_ready")
        raw_ready, max_ready, s_ready = sem("raw_ready"), sem("max_ready"), sem("s_ready")
        exp_done, z_ready, rz_ready, attn_ready = (
            sem(n) for n in ("exp_done", "z_ready", "rz_ready", "attn_ready"))
        o_ready, oT_ready, y_ready, x_added = (sem(n) for n in ("o_ready", "oT_ready", "y_ready", "x_added"))
        xn2_ready, x2_added, t2_ready, hi_ready, lo_ready, x2_ready = (
            sem(n) for n in ("xn2_ready", "x2_added", "t2_ready", "hi_ready", "lo_ready", "x2_ready"))
        ln2_step, seed_ready, newton_step, rstd2_ready = (
            sem(n) for n in ("ln2_step", "seed_ready", "newton_step", "rstd2_ready"))
        route_ready, raw_copied, rstep, rexp, comb_ready = (
            sem(n) for n in ("route_ready", "raw_copied", "rstep", "rexp", "comb_ready"))
        rneed = sem("rneed")
        up_ready, h_ready, dn_ready, acc_done = (
            sem(n) for n in ("up_ready", "h_ready", "dn_ready", "acc_done"))
        member_ready, rank_ready, slot_ready, token2_ready, table_ready = (
            sem(n) for n in ("member_ready", "rank_ready", "slot_ready", "token2_ready", "table_ready"))
        scattered, padded = sem("scattered"), sem("padded")
        xg_loaded = [sem(f"xg_loaded{i}") for i in range(NG)]
        gT_ready, xgT_ready, gup_ready, gh_ready, gdn_ready, yg_ready = (
            sem(n) for n in ("gT_ready", "xgT_ready", "gup_ready", "gh_ready", "gdn_ready", "yg_ready"))
        yg_stored = [sem(f"yg_stored{i}") for i in range(NG)]
        yk_loaded = [sem(f"yk_loaded{i}") for i in range(4)]
        zeroed = sem("zeroed")
        own_waits = sem("own_waits")
        combined, combined_half = sem("combined"), sem("combined_half")
        stored = sem("stored")

        block = stack.enter_context(nc.Block())

        @block.sync
        def _(sp):
            sp.dma_start(ctxT[:], ctx_t).then_inc(ctx_loaded, 16)
            sp.dma_start(wk[:], wk_t).then_inc(ctx_loaded, 16)
            sp.dma_start(wv[:], wv_t).then_inc(ctx_loaded, 16)
            xv = x.rearrange("(q t p) d -> q p t d", q=4, p=P)
            Xv = X[:].rearrange("p (q a) b c d -> p q (a b c) d", q=4)
            for q in range(4):
                sp.dma_start(Xv[:, q], xv[q]).then_inc(x_loaded[q], 16)
                if q == 0:
                    sp.dma_start(wq[:], wq_t).then_inc(wq_loaded, 16)
            for b in range(2):
                for half in range(2):
                    sp.dma_start(wo[64 * b:64 * b + 64, b, half, :],
                                 wo_t[64 * half:64 * half + 64, :]).then_inc(wo_loaded, 16)
            sp.dma_start(wfc_f32, wfc_t).then_inc(wfc_loaded, 16)
            sp.dma_start(cent[:], cent_t).then_inc(small_loaded, 16)
            sp.dma_start(bias8[:], rbias).then_inc(small_loaded, 16)
            sp.dma_start(wproj[:], wproj_t).then_inc(wproj_loaded, 16)
            ov = out.rearrange("(a t p) d -> p a t d", a=PAIRS, p=P)
            Xo = X[:].rearrange("p a b c d -> p a (b c) d")
            sp.wait_ge(masks, BUILT)
            sp.wait_ge(table_ready, 1)
            for e in range(EXPERTS + 1):
                n = sp.value_load(counts[0:1, e:e + 1], min_val=0, max_val=B * S) if e < EXPERTS else 0
                rows = gathered[bass.ds(n + e * REGION, GT)]
                sp.dma_start(rows.rearrange("(s p) r -> p s r", p=P), padding[:]).then_inc(padded, 16)
            sp.wait_ge(padded, 16 * (EXPERTS + 1))
            sp.wait_ge(scattered, 16 * 2 * TILES)

            def load_tile(j, k, n):
                if n is not None:
                    sp.wait_ge(yg_stored[k], 32 * n)
                    sp.sem_inc(own_waits, 1)
                row = sp.value_load(table[0:1, 1, bass.ds(j, 1)], min_val=0, max_val=EXPERTS * REGION)
                sp.dma_start(xg[:, k], gathered[bass.ds(row, GT)].rearrange("(s p) r -> p s r", p=P)
                             ).then_inc(xg_loaded[k], 16)

            for k in range(NG):
                load_tile(k, k, None)
            with sp.Fori(1, MAX_TILES // NG) as n:
                for k in range(NG):
                    load_tile(NG * n + k, k, n)

            for k in range(NG):
                sp.wait_ge(yg_stored[k], 32 * (MAX_TILES // NG))
            rv = results.rearrange("(k a t p) d -> a p k t d", k=2, a=PAIRS, p=P)
            for k in range(4):
                for c in range(2):
                    sp.dma_start(yk[:, k, c], rv[k, :, c]).then_inc(yk_loaded[k], 16)
            for a in range(PAIRS):
                sp.wait_ge(combined, a + 1)
                sp.dma_start(ov[:, a], Xo[:, a]).then_inc(stored, 16)
                if a < 4:
                    for c in range(2):
                        sp.dma_start(yk[:, a, c], rv[a + 4, :, c]).then_inc(yk_loaded[a], 16)
            sp.wait_ge(stored, 16 * PAIRS)

        @block.gpsimd
        def _(pool):
            g = nc.gpsimd
            built = [0]

            def then(ins):
                built[0] += 1
                ins.then_inc(masks, 1)
                pool.wait_ge(masks, built[0])

            then(g.memset(ident[:], 0.0))
            then(g.affine_select(out=ident[:], in_=ident[:], compare_op=ALU.not_equal, fill=1.0, base=0,
                                 pattern=[[-1, P]], channel_multiplier=1))
            then(g.memset(eps[:], EPS))
            then(g.memset(head_mask[:], 1.0))
            for lo in (0, 64):
                m = head_mask[lo:lo + 64, :]
                then(g.affine_select(out=m, in_=m, compare_op=ALU.is_ge, fill=0.0, base=0,
                                     pattern=[[-DK, HH]], channel_multiplier=1))
                then(g.affine_select(out=m, in_=m, compare_op=ALU.is_ge, fill=0.0, base=DK - 1,
                                     pattern=[[DK, HH]], channel_multiplier=-1))
            then(g.memset(wo[64:128, 0, :, :], 0.0))
            then(g.memset(wo[0:64, 1, :, :], 0.0))
            then(g.memset(negI[:], 0.0))
            assert built[0] == BASICS
            then(g.affine_select(out=negI[:], in_=negI[:], compare_op=ALU.not_equal, fill=-1.0, base=0,
                                 pattern=[[-1, P]], channel_multiplier=1))
            for i, value in enumerate((-0.5, 1.5, -1.0)):
                then(g.memset(consts[:, i], value))
            then(g.iota(iota8[:], [[-1, EXPERTS]], base=EXPERTS, channel_multiplier=0,
                        allow_small_or_imprecise_dtypes=True))
            then(g.memset(ident16[:], 0.0))
            then(g.affine_select(out=ident16[:], in_=ident16[:], compare_op=ALU.not_equal, fill=1.0, base=0,
                                 pattern=[[-1, P]], channel_multiplier=1))
            then(g.memset(ones16[:], 1.0))
            then(g.affine_select(out=before[:], in_=ones16[:], compare_op=ALU.is_gt, fill=0.0, base=0,
                                 pattern=[[1, P]], channel_multiplier=-1))
            then(g.memset(newrow[:], 1.0))
            then(g.memset(newrow[:, :, 0:1], 0.0))
            then(g.iota(region[:], [[REGION, EXPERTS], [0, TILES]], base=0, channel_multiplier=0,
                        allow_small_or_imprecise_dtypes=True))
            then(g.iota(tile_no[:], [[1, MAX_TILES], [0, EXPERTS]], base=0, channel_multiplier=0,
                        allow_small_or_imprecise_dtypes=True))
            then(g.iota(token[:], [[B * S, 2], [P, TILES]], base=0, channel_multiplier=1))
            then(g.memset(padding[:], 0.0))
            then(g.iota(padding[:, :, 2 * D:ROW].bitcast(I32), [[0, 2], [0, 1]], base=SKIP, channel_multiplier=0))
            assert built[0] == BUILT, built

            def normalise(k, u):
                pool.wait_ge(rz_ready, u + 1)
                g.tensor_tensor(E[:, k], E[:, k], rZ[:, k % 2, :].unsqueeze(1).broadcast_to([P, H, P]),
                                ALU.mult).then_inc(attn_ready, 1)

            def inverse_deviation(n):
                pool.wait_ge(seed_ready, n + 1)
                y, z = rstd2[:], newton[:]
                ops = [(z, y, y, ALU.mult), (z, z, var2[:], ALU.mult), (z, z, consts[:, 0], ALU.mult),
                       (z, z, consts[:, 1], ALU.add), (y, y, z, ALU.mult)] * 3
                ops += [(z, y, mv2[:, :, 0], ALU.mult), (shift2[:], z, consts[:, 2], ALU.mult)]
                for i, (o, a, b, op) in enumerate(ops):
                    ins = g.tensor_tensor(o, a, b, op)
                    if i < len(ops) - 1:
                        ins.then_inc(newton_step, 1)
                        pool.wait_ge(newton_step, n * (len(ops) - 1) + i + 1)
                    else:
                        ins.then_inc(rstd2_ready, 1)

            def ffn_inputs(n):
                for j in range(2):
                    pool.wait_ge(xn2_ready, 2 * n + j + 1)
                    xv = X[:, 2 * n + j].rearrange("p b c d -> p (b c) d")
                    g.tensor_tensor(xv, xv, xn[:, j], ALU.add).then_inc(x2_added, 1)
                for j in range(2):
                    tiles = bass.ds((2 * n + j) * TP, TP)
                    pool.wait_ge(hi_ready, 2 * n + j + 1)
                    g.tensor_tensor(xs[:, tiles, D:2 * D], xn[:, j], xs[:, tiles, 0:D],
                                    ALU.subtract).then_inc(lo_ready, 1)

            for k in range(4):
                normalise(k, k)
            with pool.Fori(1, UNITS // 4) as n:
                normalise(0, 4 * n)
                normalise(1, 4 * n + 1)
                inverse_deviation(n - 1)
                normalise(2, 4 * n + 2)
                normalise(3, 4 * n + 3)
                ffn_inputs(n - 1)
            inverse_deviation(PAIRS // 2 - 1)
            ffn_inputs(PAIRS // 2 - 1)

            pool.wait_ge(slot_ready, 1)
            for k in range(2):
                if k == 1:
                    pool.wait_ge(token2_ready, 1)
                for i in range(TILES):
                    g.indirect_dma_start(
                        out=gathered, out_offset=bass.IndirectOffsetOnAxis(ap=slot[:, k, i:i + 1], axis=0),
                        in_=xs[:, i, :], in_offset=None, bounds_check=EXPERTS * REGION - 1,
                        oob_is_err=False).then_inc(scattered, 16)

            with pool.Fori(0, MAX_TILES // NG) as n:
                for k in range(NG):
                    pool.wait_ge(yg_ready, NG * n + k + 1)
                    pool.sem_inc(own_waits, 1)
                    for h in range(2):
                        g.indirect_dma_start(
                            out=results,
                            out_offset=bass.IndirectOffsetOnAxis(ap=xg[:, k, h, 2 * D:ROW].bitcast(I32), axis=0),
                            in_=yg[:, k, h, :], in_offset=None, bounds_check=2 * B * S - 1,
                            oob_is_err=False).then_inc(yg_stored[k], 16)

        @block.scalar
        def _(act):
            s = nc.scalar
            for half in range(2):
                act.wait_ge(k_ready, half + 1)
                s.activation(kT[:, half], k_ps[half], ACT.Copy).then_inc(kT_ready, 1)
            for i in range(2):
                act.wait_ge(v_ready, i + 1)
                s.activation(V[:, 4 * i:4 * i + 4], v_ps[i], ACT.Copy).then_inc(V_ready, 1)
            act.wait_ge(wfc_loaded, 16)
            with act.Fori(0, NE) as e:
                s.activation(wfcH[:, e], wfc_f32[:, e], ACT.Copy, scale=W_SCALE).then_inc(wfcH_ready, 1)

            act.wait_ge(masks, BASICS)
            act.wait_ge(mv_ready, 4)
            s.activation(sd[:], mv[:, :, 1], ACT.Sqrt, bias=eps[:]).then_inc(sd_ready, 1)
            act.wait_ge(rstd_ready, 1)

            def q_side(n, again):
                if again:
                    act.wait_ge(t_ready, 2 * n)
                for i in range(TP):
                    at = bass.ds((2 * n + 1) * TP + i, 1)
                    last = s.activation(xn[:, 1, i], X[:, 2 * n + 1, i // 2, i % 2, :], ACT.Identity,
                                        bias=shift[:, at], scale=rstd[:, at])
                last.then_inc(xn1_ready, 1)
                for j in range(2):
                    act.wait_ge(t_ready, 2 * n + j + 1)
                    s.activation(xnT[:, j], t_ps[j], ACT.Copy).then_inc(xnT_ready, 1)
                for j in range(2):
                    act.wait_ge(q_ready, 2 * n + j + 1)
                    s.activation(qT[:, 2 * n + j], q_ps[j], ACT.Copy).then_inc(qT_ready, 1)

            q_side(0, False)
            with act.Fori(1, PAIRS // 2) as n:
                q_side(n, True)
            def copy_o(u, k):
                act.wait_ge(o_ready, u + 1)
                s.activation(oT[:, k % 2], o_ps[:, 0:2 * P], ACT.Copy).then_inc(oT_ready, 1)

            def exps(u, k, again):
                act.wait_ge(s_ready, u + 1)
                if again:
                    act.wait_ge(o_ready, u - 3)
                for i in range(2):
                    s.activation(E[:, k, 8 * i:8 * i + 8], scores[:, 2 * i:2 * i + 2], ACT.Exp,
                                 scale=DK ** -0.5).then_inc(exp_done, 1)

            act.wait_ge(wfcL_ready, NE)
            def second_norm(n, again):
                act.wait_ge(rstd2_ready, n + 1)
                if again:
                    act.wait_ge(lo_ready, 2 * n)
                    act.wait_ge(x2_added, 2 * n)
                for j in range(2):
                    for i in range(TP):
                        at = slice(j * TP + i, j * TP + i + 1)
                        last = s.activation(xn[:, j, i], X[:, 2 * n + j, i // 2, i % 2, :], ACT.Identity,
                                            bias=shift2[:, at], scale=rstd2[:, at])
                    last.then_inc(xn2_ready, 1)
                for j in range(2):
                    act.wait_ge(xn2_ready, 2 * n + j + 1)
                    s.activation(xs[:, bass.ds((2 * n + j) * TP, TP), 0:D], xn[:, j], ACT.Copy).then_inc(hi_ready, 1)

            for k in range(4):
                if k >= 2:
                    copy_o(k - 2, k)
                exps(k, k, False)

            def later_units(n, again):
                for k in range(4):
                    u = 4 * n
                    act.wait_ge(y_ready, u + k - 3)
                    copy_o(u + k - 2, k)
                    exps(u + k, k, True)
                second_norm(n - 1, again)

            later_units(1, False)
            with act.Fori(2, UNITS // 4) as n:
                later_units(n, True)
            for k in range(2):
                act.wait_ge(y_ready, UNITS + k - 3)
                copy_o(UNITS - 2 + k, k)

            def copy_x2(pair):
                act.wait_ge(t2_ready, pair + 1)
                s.activation(x2[:, :, bass.ds(pair * BANK, BANK)], t2_ps[pair % 2], ACT.Copy).then_inc(x2_ready, 1)

            def gelus(i, e, again):
                if again:
                    act.wait_ge(dn_ready, i - 1)
                for c in range(FC):
                    act.wait_ge(up_ready, i * FC + c + 1)
                    s.activation(hid[:, e, c], up_ps[c], ACT.Gelu, scale=1.0 / W_SCALE).then_inc(h_ready, 1)

            for pair in range(PAIRS - 2):
                copy_x2(pair)
            second_norm(PAIRS // 2 - 1, True)
            for e in range(2):
                gelus(e, e, False)
            for pair in (PAIRS - 2, PAIRS - 1):
                copy_x2(pair)
            act.wait_ge(rneed, 2)
            s.activation(rt[:, 1:3], rt[:, 1:3], ACT.Exp, scale=-1.0).then_inc(rexp, 1)
            for e in range(2):
                gelus(2 + e, e, True)
            act.wait_ge(rneed, 4)
            s.activation(r1[:, 4:6], r1[:, 4:6], ACT.Exp).then_inc(rexp, 1)
            with act.Fori(2, PAIRS) as n:
                for e in range(2):
                    gelus(2 * n + e, e, True)

            def routed_gelus(i, j, again):
                if again:
                    act.wait_ge(gdn_ready, i - 1)
                for c in range(2):
                    act.wait_ge(gup_ready, 2 * i + c + 1)
                    s.activation(hid_g[:, j, 2 * c:2 * c + 2], up_ps[2 * j + c].rearrange("p (c q) -> p c q", c=2),
                                 ACT.Gelu, scale=1.0 / W_SCALE).then_inc(gh_ready, 1)

            act.wait_ge(dn_ready, SHARED * PAIRS)
            for j in range(2):
                routed_gelus(j, j, False)
            with act.Fori(1, MAX_TILES // 2) as n:
                for j in range(2):
                    routed_gelus(2 * n + j, j, True)

        @block.vector
        def _(dve):
            v = nc.vector

            def pad_k(j, pair):
                for b in range(2):
                    r = slice(64 * b, 64 * b + 64)
                    v.tensor_tensor(kPad[r, j, :, :, b, :],
                                    kT[r, :, pair, :].unsqueeze(2).broadcast_to([64, 2, HH, SK]),
                                    head_mask[r, :].unsqueeze(1).unsqueeze(3).broadcast_to([64, 2, HH, SK]),
                                    ALU.mult).then_inc(kPad_ready, 1)

            def spread_v(j, pair):
                for b in range(2):
                    r = slice(64 * b, 64 * b + 64)
                    dst = vPad[j][r].rearrange("p a (h s) -> p a h s", s=P + DK)[:, :, :, 64 * b:64 * b + DK]
                    src = V[r, pair, :].rearrange("p (a h d) -> p a h d", a=2, d=DK)
                    v.tensor_copy(dst, src).then_inc(vPad_ready, 1)

            v.memset(kPad[:, 0], 0.0).then_inc(zeroed, 1)
            v.memset(kPad[:, 1], 0.0).then_inc(zeroed, 1)
            v.memset(vPad[0][:], 0.0).then_inc(zeroed, 1)
            v.memset(vPad[1][:], 0.0).then_inc(zeroed, 1)
            dve.wait_ge(zeroed, 4)
            dve.wait_ge(masks, BASICS)
            dve.wait_ge(kT_ready, 2)
            pad_k(0, 0)
            for q in range(4):
                dve.wait_ge(x_loaded[q], 16)
                own = range(8 * q, 8 * q + 8)
                for i in own:
                    last = v.bn_stats(stats1[:, i, :], X[:, i // 4, i // 2 % 2, i % 2, :])
                last.then_inc(ln_step, 1)
                dve.wait_ge(ln_step, q + 1)
                for i in own:
                    last = v.bn_aggr(mv[:, i, :], stats1[:, i, :])
                last.then_inc(mv_ready, 1)
            dve.wait_ge(sd_ready, 1)
            v.reciprocal(rstd[:], sd[:]).then_inc(ln_step, 1)
            dve.wait_ge(ln_step, 5)
            v.scalar_tensor_tensor(shift[:], mv[:, :, 0], -1.0, rstd[:], ALU.mult, ALU.mult).then_inc(rstd_ready, 1)

            def first_norm(n, again):
                if again:
                    dve.wait_ge(t_ready, 2 * n - 1)
                for i in range(TP):
                    at = (2 * n) * TP + i
                    last = v.tensor_scalar(xn[:, 0, i], X[:, 2 * n, i // 2, i % 2, :], mv[:, bass.ds(at, 1), 0],
                                           rstd[:, bass.ds(at, 1)], ALU.subtract, ALU.mult)
                last.then_inc(xn_ready, 1)

            first_norm(0, False)
            pad_k(1, 1)
            dve.wait_ge(V_ready, 2)
            spread_v(0, 0)
            spread_v(1, 1)
            with dve.Fori(1, PAIRS // 2) as n:
                first_norm(n, True)
            with dve.Fori(0, NE) as e:
                dve.wait_ge(wfcH_ready, e + 1)
                v.scalar_tensor_tensor(wfcL[:, e], wfc_f32[:, e], W_SCALE, wfcH[:, e],
                                       ALU.mult, ALU.subtract).then_inc(wfcL_ready, 1)

            def second_stats(n, again):
                dve.wait_ge(x_added, 4 * n + 4)
                for i in range(2 * TP):
                    last = v.bn_stats(stats[:, i, :], X[:, 2 * n + i // TP, i // 2 % 2, i % 2, :])
                last.then_inc(ln2_step, 1)
                if again:
                    dve.wait_ge(xn2_ready, 2 * n)
                    dve.sem_inc(own_waits, 1)
                dve.wait_ge(ln2_step, 3 * n + 1)
                dve.sem_inc(own_waits, 1)
                for i in range(2 * TP):
                    last = v.bn_aggr(mv2[:, i, :], stats[:, i, :])
                last.then_inc(ln2_step, 1)
                dve.wait_ge(ln2_step, 3 * n + 2)
                v.tensor_scalar(var2[:], mv2[:, :, 1], EPS, None, ALU.add).then_inc(ln2_step, 1)
                dve.wait_ge(ln2_step, 3 * n + 3)
                v.tensor_scalar(rstd2[:].bitcast(I32), var2[:].bitcast(I32), -0.5, float(0x5f3759df),
                                ALU.mult, ALU.add).then_inc(seed_ready, 1)

            def max_heads(u, k):
                dve.wait_ge(raw_ready, u + 1)
                v.tensor_reduce(Mx[:, k % 2, :], scores.rearrange("p b (h q) -> p q (b h)", q=P),
                                AX_X, ALU.max).then_inc(max_ready, 1)

            def sum_heads(u, k):
                dve.wait_ge(exp_done, 2 * u + 2)
                v.tensor_reduce(Z[:, k % 2, :], E[:, k].rearrange("p h q -> p q h"), AX_X,
                                ALU.add).then_inc(z_ready, 1)
                dve.wait_ge(z_ready, u + 1)
                v.reciprocal(rZ[:, k % 2, :], Z[:, k % 2, :]).then_inc(rz_ready, 1)

            def add_attention(u, qh, pair):
                dve.wait_ge(y_ready, u + 1)
                v.tensor_tensor(X[:, pair, :, qh, :], X[:, pair, :, qh, :],
                                y_ps[:, 0:2 * D].rearrange("p (b d) -> p b d", b=2), ALU.add).then_inc(x_added, 1)

            def four_units(n, first, second, last):
                u, pair = 4 * n, 2 * n
                for k in range(4):
                    if not (first and k == 0):
                        if not (first and k < 3):
                            dve.wait_ge(attn_ready, u + k - 2)
                        sum_heads(u + k - 1, (k - 1) % 4)
                    if not (first and k < 3):
                        kk = k - 3
                        add_attention(u + kk, kk % 2, pair + (kk // 2))
                        if kk % 2 == 1:
                            spread_v((kk // 2) % 2, pair + kk // 2 + 2)
                        if kk == -1:
                            second_stats(n - 1, not second)
                    max_heads(u + k, k)
                    if k % 2 == 1 and not last:
                        pad_k(k // 2, pair + k // 2 + 2)

            four_units(0, True, False, False)
            four_units(1, False, True, False)
            with dve.Fori(2, PAIRS // 2 - 1) as n:
                four_units(n, False, False, False)
            four_units(PAIRS // 2 - 1, False, False, True)
            dve.wait_ge(attn_ready, UNITS - 2)
            sum_heads(UNITS - 1, 3)
            for k in (1, 2, 3):
                add_attention(UNITS - 4 + k, k % 2, PAIRS - 2 + k // 2)
            second_stats(PAIRS // 2 - 1, True)

            dve.wait_ge(small_loaded, 32)
            v.tensor_copy(centH[:], cent[:]).then_inc(rstep, 1)
            dve.wait_ge(rstep, 1)
            v.tensor_tensor(centL[:], cent[:], centH[:], ALU.subtract).then_inc(rstep, 1)

            def copy_raw(pair):
                dve.wait_ge(route_ready, pair + 1)
                v.tensor_copy(rt[:, 0, pair * TP:pair * TP + TP, :],
                              r_ps[pair % 2][:, 0:TP * EXPERTS].rearrange("p (t e) -> p t e", e=EXPERTS)
                              ).then_inc(raw_copied, 1)

            def add_shared(pair, j):
                dve.wait_ge(dn_ready, SHARED * pair + SHARED)
                xv = X[:, pair].rearrange("p b c d -> p (b c d)")
                v.tensor_tensor(xv, xv, dn_ps[j], ALU.add).then_inc(acc_done, 1)

            for pair in range(PAIRS - 2):
                copy_raw(pair)
            dve.wait_ge(x2_added, PAIRS)
            add_shared(0, 0)
            for pair in (PAIRS - 2, PAIRS - 1):
                copy_raw(pair)

            steps = [2]

            def then(ins):
                steps[0] += 1
                ins.then_inc(rstep, 1)
                dve.wait_ge(rstep, steps[0])

            def all8(t):
                return t.unsqueeze(2).broadcast_to([P, TILES, EXPERTS])

            tok8 = [P, TILES, EXPERTS]
            iota_b = iota8[:].unsqueeze(1).broadcast_to(tok8)
            dve.wait_ge(raw_copied, PAIRS)
            v.tensor_copy(rt[:, 1], rt[:, 0]).then_inc(rneed, 1)
            v.tensor_tensor(rt[:, 2], rt[:, 0], bias8[:].unsqueeze(1).broadcast_to(tok8), ALU.add).then_inc(rneed, 1)
            dve.wait_ge(rexp, 1)
            then(v.tensor_scalar(rt[:, 1:3], rt[:, 1:3], 1.0, None, ALU.add))
            then(v.reciprocal(rt[:, 3:5], rt[:, 1:3]))
            sig, bal = rt[:, 3], rt[:, 4]

            def pick(scores_, slot, k):
                then(v.tensor_reduce(r1[:, k], scores_, AX_X, ALU.max))
                then(v.tensor_tensor(rt[:, slot], scores_, all8(r1[:, k]), ALU.is_equal))
                then(v.tensor_tensor(rt[:, slot], rt[:, slot], iota_b, ALU.mult))
                then(v.tensor_reduce(r1[:, k + 1], rt[:, slot], AX_X, ALU.max))
                then(v.tensor_tensor(rt[:, slot + 1], rt[:, slot], all8(r1[:, k + 1]), ALU.is_equal))

            pick(bal, 5, 0)
            then(v.scalar_tensor_tensor(rt[:, 7], rt[:, 6], -4.0, bal, ALU.mult, ALU.add))
            pick(rt[:, 7], 8, 2)
            for n, hot in enumerate((6, 9)):
                then(v.tensor_tensor(rt[:, 10 + n], rt[:, hot], sig, ALU.mult))
                then(v.tensor_reduce(r1[:, 4 + n], rt[:, 10 + n], AX_X, ALU.add))
            then(v.tensor_tensor(r1[:, 6], r1[:, 4], r1[:, 5], ALU.max))
            v.tensor_tensor(r1[:, 4], r1[:, 4], r1[:, 6], ALU.subtract).then_inc(rneed, 1)
            v.tensor_tensor(r1[:, 5], r1[:, 5], r1[:, 6], ALU.subtract).then_inc(rneed, 1)

            hot = [rt[:, 6], rt[:, 9]]
            v.tensor_tensor(member[:].rearrange("p e t -> p t e"), hot[0], hot[1], ALU.add).then_inc(member_ready, 1)
            dve.wait_ge(rank_ready, 1)
            cum = rt[:, 10].rearrange("p t e -> p (t e)").rearrange("p (e t) -> p e t", e=EXPERTS)
            tot = rt[:, 11].rearrange("p t e -> p (t e)").rearrange("p (e t) -> p e t", e=EXPERTS)
            then(v.tensor_copy(tot, tot_ps))
            then(v.tensor_tensor_scan(rt[:, 10].rearrange("p t e -> p (t e)"), newrow[:].rearrange("p e t -> p (e t)"),
                                      rt[:, 11].rearrange("p t e -> p (t e)"), 0.0, ALU.mult, ALU.add))
            then(v.tensor_copy(counts[:], cum[:, :, TILES - 1]))
            then(v.tensor_tensor(cum, cum, tot, ALU.subtract))
            then(v.tensor_tensor(cum, cum, rank_ps, ALU.add))
            then(v.tensor_tensor(cum, cum, region[:], ALU.add))
            for k in range(2):
                then(v.tensor_tensor(rt[:, 5], hot[k], cum.rearrange("p e t -> p t e"), ALU.mult))
                then(v.tensor_reduce(r1[:, 9], rt[:, 5], AX_X, ALU.add))
                then(v.tensor_copy(slot[:, k], r1[:, 9]))
            then(v.tensor_copy(xs[:, :, 2 * D:ROW].bitcast(I32), token[:, 0].unsqueeze(2)))
            v.tensor_copy(r1[:, 9, 0:EXPERTS], counts[:]).then_inc(slot_ready, 1)
            dve.wait_ge(slot_ready, 1)

            nt, end = r1[:, 10, 0:EXPERTS], r1[:, 11, 0:EXPERTS]
            then(v.tensor_scalar(tiles_of[:], r1[:, 9, 0:EXPERTS], float(GT - 1), None, ALU.add))
            then(v.tensor_scalar(tiles_of[:], tiles_of[:], GT.bit_length() - 1, None, ALU.logical_shift_right))
            then(v.tensor_copy(nt, tiles_of[:]))
            then(v.tensor_copy(end, nt))
            for e in range(1, EXPERTS):
                then(v.tensor_tensor(end[:, e:e + 1], end[:, e - 1:e], nt[:, e:e + 1], ALU.add))
            wide = [P, MAX_TILES, EXPERTS]
            passed = rt[:, 0:2].rearrange("p a t e -> p (a t e)")[:, 0:MAX_TILES * EXPERTS].rearrange(
                "p (j e) -> p j e", e=EXPERTS)
            spent = rt[:, 2:4].rearrange("p a t e -> p (a t e)")[:, 0:MAX_TILES * EXPERTS].rearrange(
                "p (j e) -> p j e", e=EXPERTS)
            tj = rt[:, 7].rearrange("p t e -> p (t e)")
            ej, sj, rj = (tj[:, i * MAX_TILES:(i + 1) * MAX_TILES] for i in range(3))
            then(v.tensor_tensor(passed, tile_no[:], end.unsqueeze(1).broadcast_to(wide), ALU.is_ge))
            then(v.tensor_tensor(spent, passed, nt.unsqueeze(1).broadcast_to(wide), ALU.mult))
            then(v.tensor_reduce(ej, passed, AX_X, ALU.add))
            then(v.tensor_reduce(sj, spent, AX_X, ALU.add))
            then(v.tensor_tensor(rj, tile_no[:, :, 0], sj, ALU.subtract))
            then(v.tensor_scalar(rj, rj, float(GT), None, ALU.mult))
            then(v.scalar_tensor_tensor(rj, ej, float(REGION), rj, ALU.mult, ALU.add))
            then(v.tensor_scalar(table[:, 1], rj, float(EXPERTS * REGION), None, ALU.min))
            v.tensor_scalar(table[:, 0], ej, float(EXPERTS - 1), None, ALU.min).then_inc(table_ready, 1)

            dve.wait_ge(rexp, 2)
            then(v.tensor_tensor(r1[:, 7], r1[:, 4], r1[:, 5], ALU.add))
            then(v.reciprocal(r1[:, 8], r1[:, 7]))
            for n in range(2):
                then(v.tensor_tensor(gate[:, n], r1[:, 4 + n], r1[:, 8], ALU.mult))

            for a in range(1, 4):
                add_shared(a, a % 2)
            dve.wait_ge(scattered, 16 * TILES)
            v.tensor_copy(xs[:, :, 2 * D:ROW].bitcast(I32), token[:, 1].unsqueeze(2)).then_inc(token2_ready, 1)
            for a in range(4, PAIRS):
                add_shared(a, a % 2)

            def routed_copies(i, k, again):
                dve.wait_ge(gT_ready, i + 1)
                if again:
                    dve.wait_ge(gup_ready, 2 * i - 2)
                v.tensor_copy(xgT[:, k % 2], g_ps[k % 2]).then_inc(xgT_ready, 1)

            def results_out(i, k, n):
                dve.wait_ge(gdn_ready, i + 1)
                if n is not None:
                    dve.wait_ge(yg_stored[k], 32 * n)
                v.tensor_copy(yg[:, k].rearrange("p s d -> p (s d)"), dn_ps[k % 2][:, 0:2 * D]).then_inc(yg_ready, 1)

            routed_copies(0, 0, False)
            for k in range(NG):
                routed_copies(k + 1, k + 1, k > 0)
                results_out(k, k, None)
            with dve.Fori(1, MAX_TILES // NG - 1) as n:
                for k in range(NG):
                    routed_copies(NG * n + k + 1, k + 1, True)
                    results_out(NG * n + k, k, n)
            for k in range(NG):
                if k < NG - 1:
                    routed_copies(MAX_TILES - NG + k + 1, k + 1, True)
                results_out(MAX_TILES - NG + k, k, MAX_TILES // NG - 1)

            for a in range(PAIRS):
                dve.wait_ge(yk_loaded[a % 4], 32 * (a // 4 + 1))
                for c in range(2):
                    for i in range(TP):
                        xv = X[:, a, i // 2, i % 2, :]
                        last = v.scalar_tensor_tensor(xv, yk[:, a % 4, c, i], gate[:, c, a * TP + i:a * TP + i + 1], xv,
                                                      ALU.mult, ALU.add)
                    last.then_inc(combined_half if c == 0 else combined, 1)
                    if c == 0:
                        dve.wait_ge(combined_half, a + 1)

        @block.tensor
        def _(pe):
            t = nc.tensor
            pe.wait_ge(ctx_loaded, 48)
            for half in range(2):
                for b in range(2):
                    last = t.matmul(k_ps[half][64 * b:64 * b + 64, :], wk[:, 64 * half:64 * half + 64],
                                    ctxT[:, :, b], start=True, stop=True)
                last.then_inc(k_ready, 1)
            for i in range(2):
                for p in range(4):
                    last = t.matmul(v_ps[i][:, D * p:D * p + D], ctxT[:, 4 * i + p].rearrange("p b s -> p (b s)"), wv[:],
                                    start=True, stop=True)
                last.then_inc(v_ready, 1)

            pe.wait_ge(masks, BASICS)
            pe.wait_ge(wq_loaded, 16)

            def q_side(half_pair, again):
                pair = 2 * half_pair
                for j in range(2):
                    pe.wait_ge((xn_ready, xn1_ready)[j], half_pair + 1)
                    if again:
                        pe.wait_ge(xnT_ready, pair + j - 1)
                    for i in range(TP):
                        last = t.transpose(t_ps[j][:, P * i:P * i + P], xn[:, j, i, :], ident[:])
                    last.then_inc(t_ready, 1)
                for j in range(2):
                    pe.wait_ge(xnT_ready, pair + j + 1)
                    if again:
                        pe.wait_ge(qT_ready, pair + j - 1)
                    for half in range(2):
                        for b in range(2):
                            last = t.matmul(q_ps[j][64 * b:64 * b + 64, S * half:S * half + S],
                                            wq[:, 64 * half:64 * half + 64], xnT[:, j, S * b:S * b + S],
                                            start=True, stop=True)
                    last.then_inc(q_ready, 1)

            q_side(0, False)
            with pe.Fori(1, PAIRS // 2) as n:
                q_side(n, True)
            pe.wait_ge(masks, BUILT)

            def raw_scores(u, k, pair, first):
                for i in range(4):
                    if not first and i % 2 == 0:
                        pe.wait_ge(exp_done, 2 * u + i // 2 - 1)
                    for h in range(4 * i, 4 * i + 4):
                        last = t.matmul(scores[:, i, P * (h % 4):P * (h % 4) + P],
                                        kPad[:, (k // 2) % 2, h // HH, h % HH].rearrange("p b s -> p (b s)"),
                                        qT[:, pair, h // HH, P * (k % 2):P * (k % 2) + P],
                                        start=(h % 4 == 0), stop=False, skip_group_check=True)
                last.then_inc(raw_ready, 1)

            def minus_max(u, k):
                pe.wait_ge(max_ready, u + 1)
                for i in range(4):
                    last = t.matmul(scores[:, i, :], negI[:], Mx[:, k % 2, :].unsqueeze(1).broadcast_to([P, 4, P]),
                                    start=False, stop=True, skip_group_check=True)
                last.then_inc(s_ready, 1)

            def weighted_values(u, k, first):
                pe.wait_ge(attn_ready, u + 1)
                if not first:
                    pe.wait_ge(oT_ready, u)
                for half in range(2):
                    for h in range(HH):
                        last = t.matmul(o_ps[:, P * half:P * half + P],
                                        vPad[k // 2][:, half, h * P:(h + 1) * P],
                                        E[:, k, half * HH + h, :], start=(h == 0), stop=(h == HH - 1))
                last.then_inc(o_ready, 1)

            def project_out(u, k, first):
                pe.wait_ge(oT_ready, u + 1)
                if not first:
                    pe.wait_ge(x_added, u)
                for b in range(2):
                    for half in range(2):
                        last = t.matmul(y_ps[:, D * b:D * b + D], oT[:, k % 2, half], wo[:, b, half],
                                        start=(half == 0), stop=(half == 1))
                last.then_inc(y_ready, 1)

            pe.wait_ge(wo_loaded, 64)
            pe.wait_ge(V_ready, 2)
            pe.wait_ge(kT_ready, 2)

            def four_units(u, pair, first):
                for k in range(4):
                    if not (first and k >= 2):
                        pass
                    if k % 2 == 0:
                        pe.wait_ge(kPad_ready, 2 * pair + k + 2)
                    raw_scores(u + k, k, pair + k // 2, first and k == 0)
                    if not (first and k < 2):
                        if k % 2 == 0:
                            pe.wait_ge(vPad_ready, u + k)
                        weighted_values(u + k - 2, (k - 2) % 4, first and k == 2)
                    minus_max(u + k, k)
                    if not (first and k < 2):
                        project_out(u + k - 2, (k - 2) % 4, first and k == 2)

            four_units(0, 0, True)
            with pe.Fori(1, PAIRS // 2) as n:
                four_units(4 * n, 2 * n, False)
            pe.wait_ge(vPad_ready, 2 * PAIRS)
            for k in (2, 3):
                weighted_values(UNITS - 4 + k, k, False)
                project_out(UNITS - 4 + k, k, False)

            pe.wait_ge(rstep, 2)

            def ffn_side(pair, again):
                for j in range(2):
                    pe.wait_ge(hi_ready, pair + j + 1)
                    pe.wait_ge(lo_ready, pair + j + 1)
                    if again:
                        pe.wait_ge(x2_ready, pair + j - 1)
                    for l in range(2):
                        for i in range(TP):
                            last = t.matmul(t2_ps[j][:, l, P * i:P * i + P],
                                            xs[:, (pair + j) * TP + i, D * l:D * l + D], ident16[:],
                                            start=True, stop=True)
                    last.then_inc(t2_ready, 1)
                for j in range(2):
                    pe.wait_ge(x2_ready, pair + j + 1)
                    if again:
                        pe.wait_ge(raw_copied, pair + j - 1)
                    for i in range(TP):
                        tok = bass.ds((pair + j) * BANK + P * i, P)
                        o = r_ps[j][:, EXPERTS * i:EXPERTS * i + EXPERTS]
                        t.matmul(o, x2[:, 0, tok], centL[:], start=True, stop=False)
                        t.matmul(o, x2[:, 1, tok], centH[:], start=False, stop=False)
                        last = t.matmul(o, x2[:, 0, tok], centH[:], start=False, stop=True)
                    last.then_inc(route_ready, 1)

            ffn_side(0, False)
            with pe.Fori(1, PAIRS // 2 - 1) as n:
                ffn_side(2 * n, True)

            pe.wait_ge(wproj_loaded, 16)
            pe.wait_ge(wfcL_ready, NE)

            def shared_expert(pair, j, e, i, again, dn_reused=False):
                def up(c):
                    if again or e:
                        pe.wait_ge(h_ready, i * FC + c - 3)
                    f = slice(c * P, c * P + P)
                    tok = bass.ds(pair * BANK, BANK)
                    t.matmul(up_ps[c], wfcH[:, e, f], x2[:, 1, tok], start=True, stop=False)
                    t.matmul(up_ps[c], wfcL[:, e, f], x2[:, 0, tok], start=False, stop=False)
                    t.matmul(up_ps[c], wfcH[:, e, f], x2[:, 0, tok], start=False, stop=True).then_inc(up_ready, 1)

                def down(c):
                    pe.wait_ge(h_ready, i * FC + c + 1)
                    if c == 0 and e == 0 and dn_reused:
                        pe.wait_ge(acc_done, pair - 1)
                    for q in range(TP):
                        last = t.matmul(dn_ps[j][:, P * q:P * q + P], hid[:, e, c, P * q:P * q + P],
                                        wproj[:, e, c], start=(e == 0 and c == 0 and q == 0),
                                        stop=(e == 1 and c == FC - 1), skip_group_check=True)
                    return last

                up(0), up(1), up(2)
                down(0)
                up(3)
                down(1), down(2)
                down(3).then_inc(dn_ready, 1)

            pe.wait_ge(x2_ready, PAIRS - 2)
            for e in range(SHARED):
                shared_expert(0, 0, e, e, e == 1)
            ffn_side(PAIRS - 2, True)
            pe.wait_ge(x2_ready, PAIRS)
            shared_expert(1, 1, 0, 2, True)
            pe.wait_ge(member_ready, 1)
            t.matmul(rank_ps, before[:], member[:], start=True, stop=True)
            t.matmul(tot_ps, ones16[:], member[:], start=True, stop=True).then_inc(rank_ready, 1)
            shared_expert(1, 1, 1, 3, True)
            with pe.Fori(1, PAIRS // 2) as n:
                for j in range(2):
                    for e in range(SHARED):
                        shared_expert(2 * n + j, j, e, (2 * n + j) * SHARED + e, True, True)

            def gather_transpose(i, k, n, first_two=False):
                pe.wait_ge(xg_loaded[k], 16 * n + 16)
                if not first_two:
                    pe.wait_ge(xgT_ready, i - 1)
                for l in range(2):
                    for h in range(2):
                        last = t.transpose(g_ps[k % 2][:, l, P * h:P * h + P], xg[:, k, h, D * l:D * l + D], ident16[:])
                last.then_inc(gT_ready, 1)

            def routed_up(i, k, first):
                j = k % 2
                e = pe.value_load(table[0:1, 0, bass.ds(i, 1)], min_val=0, max_val=EXPERTS - 1) + SHARED
                pe.wait_ge(xgT_ready, i + 1)
                for c in range(FC):
                    if not first and c % 2 == 0:
                        pe.wait_ge(gh_ready, 2 * i + c // 2 - 3)
                    o = up_ps[2 * j + c // 2][:, GT * (c % 2):GT * (c % 2) + GT]
                    f = bass.ds(c * P, P)
                    t.matmul(o, wfcH[:, e, f], xgT[:, j, 1], start=True, stop=False)
                    t.matmul(o, wfcL[:, e, f], xgT[:, j, 0], start=False, stop=False)
                    last = t.matmul(o, wfcH[:, e, f], xgT[:, j, 0], start=False, stop=True)
                    if c % 2:
                        last.then_inc(gup_ready, 1)

            def routed_down(i, k, first):
                j = k % 2
                e = pe.value_load(table[0:1, 0, bass.ds(i, 1)], min_val=0, max_val=EXPERTS - 1) + SHARED
                pe.wait_ge(gh_ready, 2 * i + 2)
                if not first:
                    pe.wait_ge(yg_ready, i - 1)
                for h in range(2):
                    for c in range(FC):
                        last = t.matmul(dn_ps[j][:, P * h:P * h + P], hid_g[:, j, c, P * h:P * h + P],
                                        wproj[:, e, c], start=(c == 0), stop=(c == FC - 1))
                last.then_inc(gdn_ready, 1)

            pe.wait_ge(table_ready, 1)
            pe.wait_ge(acc_done, PAIRS)
            pe.wait_ge(h_ready, SHARED * PAIRS * FC)
            gather_transpose(0, 0, 0, True)
            for k in range(NG):
                gather_transpose(k + 1, (k + 1) % NG, 0 if k < NG - 1 else 1, k == 0)
                routed_up(k, k, k < 2)
                if k:
                    routed_down(k - 1, k - 1, k < 3)
            with pe.Fori(1, MAX_TILES // NG - 1) as n:
                for k in range(NG):
                    gather_transpose(NG * n + k + 1, (k + 1) % NG, n if k < NG - 1 else n + 1)
                    routed_up(NG * n + k, k, False)
                    routed_down(NG * n + k - 1, (k - 1) % NG, False)
            m = MAX_TILES // NG - 1
            for k in range(NG):
                if k < NG - 1:
                    gather_transpose(NG * m + k + 1, k + 1, m)
                routed_up(NG * m + k, k, False)
                routed_down(NG * m + k - 1, (k - 1) % NG, False)
            routed_down(MAX_TILES - 1, NG - 1, False)


def kernel(**inputs):
    import concourse.bacc as bacc
    from concourse.bass_utils import run_bass_kernel_spmd

    f32 = {k: np.asarray(v) for k, v in inputs.items()}
    arrays = {
        "x": f32["x"].reshape(B * S, D),
        "ctx_t": f32["ctx_1024"].reshape(PAIRS, 2, SK, D).transpose(3, 0, 1, 2),
        "wq_t": f32["L0_xattn_Wq"].T,
        "wk_t": f32["L0_xattn_Wk"].T,
        "wv_t": f32["L0_xattn_Wv"].T,
        "wo_t": f32["L0_xattn_Wo"].T,
        "cent_t": f32["L0_ffn_centroids"].T,
        "rbias": np.broadcast_to(f32["L0_ffn_routing_bias"], (P, EXPERTS)),
        "wfc_t": np.concatenate([f32["L0_ffn_Wfc_sh"], f32["L0_ffn_Wfc_r"]]).transpose(2, 0, 1),
        "wproj_t": np.concatenate([f32["L0_ffn_Wproj_sh"], f32["L0_ffn_Wproj_r"]])
                     .reshape(NE, D, FC, P).transpose(3, 0, 2, 1),
    }
    nc = bacc.Bacc("TRN2", target_bir_lowering=False, num_devices=1)
    arrays = {f"in_{k}": np.ascontiguousarray(a) for k, a in arrays.items()}
    aps = [nc.dram_tensor(k, a.shape, mybir.dt.from_np(a.dtype), kind="ExternalInput").ap()
           for k, a in arrays.items()]
    out = nc.dram_tensor("out", (B * S, D), F32, kind="ExternalOutput").ap()
    gathered = nc.dram_tensor("gathered", (EXPERTS * REGION + GT, ROW), F16, kind="Internal").ap()
    results = nc.dram_tensor("results", (2 * B * S, D), F32, kind="Internal").ap()
    xattn_moe_kernel(nc, *aps, out, gathered, results)
    r = run_bass_kernel_spmd(nc, [arrays], core_ids=[0])
    return r.results[0]["out"].reshape(B, S, D)
```

```python
import numpy as np
from contextlib import ExitStack

import concourse.bass as bass
from concourse import mybir

F32 = mybir.dt.float32
F16 = mybir.dt.float16
I32 = mybir.dt.int32
BF16 = mybir.dt.bfloat16
ALU = mybir.AluOpType
ACT = mybir.ActivationFunctionType
AX_X = mybir.AxisListType.X

P = 128
D = 128
B, S, SK = 16, 256, 64
H, DK = 16, 8
HH = H // 2
PAIRS = B // 2
TILES = B * S // P
TP = TILES // PAIRS
UNITS = 2 * PAIRS
EXPERTS, SHARED = 8, 2
NE = EXPERTS + SHARED
F = 4 * D
FC = F // P
EPS = 1e-5
W_SCALE = 64.0
REGION = B * S + 2 * P
GT = 2 * P
MAX_TILES = (2 * B * S + EXPERTS * (GT - 1)) // GT
ROW = 2 * D + 2
NG = 8
ROUNDS, REST = divmod(MAX_TILES, NG)
LATE = PAIRS // 2
PORTIONS = ((0, TILES - 2 * TP), (TILES - 2 * TP, TILES))
PROJ_PARTS = ((0, 4), (4, 9), (9, NE))
LN2_STEPS = 5
BASICS, BUILT = 10, 26
QUARTER = 4
SKIP = 1 << 20
NBANK = 8
BANK = 512


def xattn_moe_kernel(nc, x, ctx_t, wq_t, wk_t, wv_t, wo_t, cent_t, rbias, wfc_t, wproj_t, out, gathered, results):
    with ExitStack() as stack:
        def sb(name, shape, dt=F32):
            return stack.enter_context(nc.sbuf_tensor(name, shape, dt))

        def sem(name):
            return stack.enter_context(nc.semaphore(name))

        X = sb("X", [P, PAIRS, 2, 2, D])
        wo = sb("wo", [P, 2, 2, D])
        cent = sb("cent", [P, EXPERTS])
        centH = sb("centH", [P, EXPERTS], F16)
        centL = sb("centL", [P, EXPERTS], F16)
        bias8 = sb("bias8", [P, EXPERTS])
        ident = sb("ident", [P, P])
        negI = sb("negI", [P, P], BF16)
        stripe = sb("stripe", [P, 2, 2 * QUARTER])
        head_mask = sb("head_mask", [P, 2, 2])
        eps = sb("eps", [P, 1])
        zero = sb("zero", [P, 1])
        V = sb("V", [P, PAIRS, D])
        kRep = sb("kRep", [P, HH, PAIRS, SK], F16)
        kPad = sb("kPad", [P, 2, H, 2, SK], F16)
        vPad = [sb(f"vPad{j}", [P, 2, HH * (P + DK)]) for j in range(2)]
        qRep = sb("qRep", [P, PAIRS, HH, S], F16)
        xn = sb("xn", [P, 2, TP, D])
        mv = sb("mv", [P, TILES, 2])
        sd = sb("sd", [P, TILES])
        rstd = sb("rstd", [P, TILES])
        shift = sb("shift", [P, TILES])
        stats = sb("stats", [P, 2 * TP, 6])
        mv2 = sb("mv2", [P, 2 * TP, 2])
        var2 = sb("var2", [P, 2 * TP])
        newton = sb("newton", [P, 2 * TP])
        rstd2 = sb("rstd2", [P, 2 * TP])
        rstd2p1 = sb("rstd2p1", [P, 2 * TP])
        half_var, neg_mean = sb("half_var", [P, 2 * TP]), sb("neg_mean", [P, 2 * TP])
        shift2 = sb("shift2", [P, 2 * TP])
        consts = sb("consts", [P, 3, 2 * TP])
        xs = sb("xs", [P, TILES, ROW], F16)
        Mx = sb("Mx", [P, 2, P], BF16)
        Z = sb("Z", [P, 2, P])
        rZ = sb("rZ", [P, 2, P])
        E = sb("E", [P, 4, H, P])
        oT = sb("oT", [P, 2, 2, P])
        x2 = sb("x2", [P, 2, TILES * P], F16)
        wfcH = sb("wfcH", [P, NE, F], F16)
        wfcL = sb("wfcL", [P, NE, F], F16)
        wprojH = sb("wprojH", [P, NE, FC * D], F16)
        wprojL = sb("wprojL", [P, NE, FC * D], F16)
        gate = sb("gate", [P, 2, TILES])
        ident16 = sb("ident16", [P, P], F16)
        before = sb("before", [P, P], BF16)
        ones16 = sb("ones16", [P, P], BF16)
        member = sb("member", [P, EXPERTS, TILES], BF16)
        newrow = sb("newrow", [P, EXPERTS, TILES])
        region = sb("region", [P, EXPERTS, TILES])
        tile_no = sb("tile_no", [P, MAX_TILES, EXPERTS])
        slot = sb("slot", [P, 2, TILES], I32)
        token = sb("token", [P, 2, TILES], I32)
        counts = sb("counts", [P, EXPERTS], I32)
        tiles_of = sb("tiles_of", [P, EXPERTS], I32)
        table = sb("table", [P, 2, MAX_TILES], I32)
        kPad_flat = kPad[:].rearrange("p j h b s -> p (j h b s)")
        padding = kPad_flat[:, 0:2 * ROW].rearrange("p (s r) -> p s r", s=2)
        x2_flat = x2[:].rearrange("p l t -> p (l t)")
        x2_rest = x2_flat[:, B * S:].bitcast(F32)
        ctxT = x2_rest[:, 0:B * SK].rearrange("p (a b s) -> p a b s", a=PAIRS, b=2)
        xnT = x2_rest[:, B * SK:B * SK + 2 * TP * P].rearrange("p (j t) -> p j t", j=2)
        q_flat = qRep[:].rearrange("p a g q -> p (a g q)")
        xg = q_flat[:, 0:NG * 2 * ROW].rearrange("p (k s r) -> p k s r", k=NG, s=2)
        xgT = q_flat[:, NG * 2 * ROW:NG * 2 * ROW + 4 * GT].rearrange("p (k l q) -> p k l q", k=2, l=2)
        yk = q_flat.bitcast(F32).rearrange("p (a k t d) -> p a k t d", a=PAIRS, k=2, t=TP)
        yg = vPad[0][:].rearrange("p a s -> p (a s)")[:, 0:NG * 2 * D].rearrange("p (k s d) -> p k s d", k=NG, s=2)
        E_flat = E[:].rearrange("p a h q -> p (a h q)")
        wfc_f32 = E_flat[:, 0:NE * F].rearrange("p (e f) -> p e f", e=NE)
        NR = 12
        rt = E_flat[:, 0:NR * TILES * EXPERTS].rearrange("p (n t e) -> p n t e", n=NR, t=TILES)
        k_flat = kRep[:].rearrange("p g a s -> p (g a s)")
        hid = k_flat.bitcast(F32).rearrange("p (c n) -> p c n", c=FC)
        hidH, hidL = (E_flat[:, 4096 + 2048 * l:6144 + 2048 * l].bitcast(F16).rearrange(
            "p (j c n) -> p j c n", j=2, c=FC) for l in (0, 1))
        r1 = kPad_flat[:, 2 * ROW:2 * ROW + 2 * 12 * TILES].bitcast(F32).rearrange("p (n t) -> p n t", n=12)
        stats1 = E_flat[:, NE * F:NE * F + TILES * 6].rearrange("p (t s) -> p t s", s=6)
        xs_flat = xs[:].rearrange("p t r -> p (t r)")
        select = xs_flat[:, 0:2 * 2 * QUARTER * P].rearrange(
            "p (w l g m) -> p w l g m", w=2, l=2, g=QUARTER)
        wq, wk, wv = (xs_flat[:, 2048 + 2 * D * i:2048 + 2 * D * i + 2 * D].bitcast(F32)
                      for i in range(3))
        ks = E_flat[:, 5376:6400].bitcast(F16).rearrange("p (l h n) -> p l h n", l=2, h=2)
        qs = E_flat[:, 6400:7424].bitcast(F16).rearrange("p (j l n) -> p j l n", j=2, l=2)
        gH, gL = (x.rearrange("p j c n -> p j (c n)")[:, :, 0:FC * GT].rearrange("p j (c n) -> p j c n", c=FC)
                  for x in (hidH, hidL))
        proj_f32 = [x2_flat[:, 0:4 * 2 * F].bitcast(F32).rearrange("p (e n) -> p e n", e=4),
                    xs_flat[:, 2816:2816 + 5 * 2 * F].bitcast(F32).rearrange("p (e n) -> p e n", e=5),
                    E_flat[:, 7424:7424 + F].rearrange("p (e n) -> p e n", e=1)]
        iota8 = sb("iota8", [P, EXPERTS])

        banks = stack.enter_context(nc.psum_tensor("banks", [P, NBANK, BANK], F32))
        k_ps = [banks[:, i, :] for i in (0, 1)]
        v_ps = [banks[:, i, :] for i in (2, 3)]
        t_ps = [banks[:, i, :] for i in (4, 5)]
        q_ps = [banks[:, i, :] for i in (6, 7)]
        spread_ps = [banks[:, 2 * i:2 * i + 2, :] for i in (0, 1)]
        scores = banks[:, 0:4, :]
        o_ps = banks[:, 4, :]
        y_ps = banks[:, 5, :]
        t2_ps = banks[:, 6:8, :]
        r_ps = banks[:, 6, :]
        rank_ps, tot_ps = (banks[:, 6, i * 256:i * 256 + 256].rearrange("p (e t) -> p e t", e=EXPERTS)
                           for i in (0, 1))
        up_ps = [banks[:, i, :] for i in (0, 1, 2, 3)]
        dn_ps = [banks[:, i, :] for i in (4, 5)]
        g_ps = [banks[:, i, 0:BANK // 2].bitcast(F16).rearrange("p (l q) -> p l q", l=2) for i in (6, 7)]

        ctx_loaded, wq_loaded, wo_loaded = sem("ctx_loaded"), sem("wq_loaded"), sem("wo_loaded")
        x_loaded = [sem(f"x_loaded{q}") for q in range(4)]
        wfc_loaded, wproj_loaded, small_loaded = sem("wfc_loaded"), sem("wproj_loaded"), sem("small_loaded")
        masks = sem("masks")
        k_ready, v_ready = sem("k_ready"), sem("v_ready")
        khi_ready, klo_ready, V_ready = sem("khi_ready"), sem("klo_ready"), sem("V_ready")
        spread = [sem(f"spread{i}") for i in range(2)]
        spread_out = [sem(f"spread_out{i}") for i in range(2)]
        mask_ready, select_ready, inv_step = sem("mask_ready"), sem("select_ready"), sem("inv_step")
        qhi_ready, qlo_ready = sem("qhi_ready"), sem("qlo_ready")
        projH_ready, projL_ready = sem("projH_ready"), sem("projL_ready")
        wfcH_ready, wfcL_ready = sem("wfcH_ready"), sem("wfcL_ready")
        ln_step = sem("ln_step")
        mv_ready, sd_ready, rstd_ready = sem("mv_ready"), sem("sd_ready"), sem("rstd_ready")
        xn_ready, xn1_ready, t_ready, xnT_ready, q_ready = (
            sem(n) for n in ("xn_ready", "xn1_ready", "t_ready", "xnT_ready", "q_ready"))
        kPad_ready, vPad_ready = sem("kPad_ready"), sem("vPad_ready")
        raw_ready, max_ready, s_ready = sem("raw_ready"), sem("max_ready"), sem("s_ready")
        exp_done, z_ready, rz_ready, attn_ready = (
            sem(n) for n in ("exp_done", "z_ready", "rz_ready", "attn_ready"))
        o_ready, oT_ready, y_ready, x_added = (sem(n) for n in ("o_ready", "oT_ready", "y_ready", "x_added"))
        xn2_ready, x2_added, t2_ready, hi_ready, lo_ready, x2_ready = (
            sem(n) for n in ("xn2_ready", "x2_added", "t2_ready", "hi_ready", "lo_ready", "x2_ready"))
        ln2_step, seed_ready, newton_step, rstd2_ready = (
            sem(n) for n in ("ln2_step", "seed_ready", "newton_step", "rstd2_ready"))
        route_ready, rstep, rneed, rexp = (sem(n) for n in ("route_ready", "rstep", "rneed", "rexp"))
        up_ready, h_ready, dn_ready, acc_done = (
            sem(n) for n in ("up_ready", "h_ready", "dn_ready", "acc_done"))
        late_ready, late_added = sem("late_ready"), sem("late_added")
        h32_ready, hlo_ready, gh32_ready, ghlo_ready = (
            sem(n) for n in ("h32_ready", "hlo_ready", "gh32_ready", "ghlo_ready"))
        member_ready, rank_ready, slot_ready, token2_ready, table_ready = (
            sem(n) for n in ("member_ready", "rank_ready", "slot_ready", "token2_ready", "table_ready"))
        scattered = [sem(f"scattered{i}") for i in range(2)]
        padding_ready, padded = sem("padding_ready"), sem("padded")
        xg_loaded = [sem(f"xg_loaded{i}") for i in range(NG)]
        gT_ready, xgT_ready, gup_ready, gh_ready, gdn_ready, yg_ready = (
            sem(n) for n in ("gT_ready", "xgT_ready", "gup_ready", "gh_ready", "gdn_ready", "yg_ready"))
        yg_stored = [sem(f"yg_stored{i}") for i in range(NG)]
        yk_loaded = [sem(f"yk_loaded{i}") for i in range(PAIRS)]
        own_waits = sem("own_waits")
        gate_ready, gated = sem("gate_ready"), sem("gated")
        combined, combined_half = sem("combined"), sem("combined_half")
        stored = sem("stored")

        block = stack.enter_context(nc.Block())

        @block.sync
        def _(sp):
            sp.dma_start(ctxT, ctx_t).then_inc(ctx_loaded, 16)
            sp.dma_start(wk, wk_t).then_inc(ctx_loaded, 16)
            sp.dma_start(wv, wv_t).then_inc(ctx_loaded, 16)
            xv = x.rearrange("(q t p) d -> q p t d", q=4, p=P)
            Xv = X[:].rearrange("p (q a) b c d -> p q (a b c) d", q=4)
            for q in range(4):
                sp.dma_start(Xv[:, q], xv[q]).then_inc(x_loaded[q], 16)
                if q == 0:
                    sp.dma_start(wq, wq_t).then_inc(wq_loaded, 16)
            for b in range(2):
                for half in range(2):
                    sp.dma_start(wo[64 * b:64 * b + 64, b, half, :],
                                 wo_t[64 * half:64 * half + 64, :]).then_inc(wo_loaded, 16)
            sp.dma_start(wfc_f32, wfc_t).then_inc(wfc_loaded, 16)
            sp.dma_start(cent[:], cent_t).then_inc(small_loaded, 16)
            sp.dma_start(bias8[:], rbias).then_inc(small_loaded, 16)
            for part, (lo, hi) in zip(proj_f32, PROJ_PARTS):
                sp.dma_start(part, wproj_t[:, lo:hi]).then_inc(wproj_loaded, 16)
            ov = out.rearrange("(a t p) d -> p a t d", a=PAIRS, p=P)
            Xo = X[:].rearrange("p a b c d -> p a (b c) d")
            sp.wait_ge(padding_ready, 2)
            sp.wait_ge(table_ready, 1)
            for e in range(EXPERTS + 1):
                n = sp.value_load(counts[0:1, e:e + 1], min_val=0, max_val=B * S) if e < EXPERTS else 0
                rows = gathered[bass.ds(n + e * REGION, GT)]
                sp.dma_start(rows.rearrange("(s p) r -> p s r", p=P), padding).then_inc(padded, 16)
            sp.wait_ge(padded, 16 * (EXPERTS + 1))
            for portion, (lo, hi) in enumerate(PORTIONS):
                sp.wait_ge(scattered[portion], 16 * 2 * (hi - lo))

            def load_tile(j, k, n):
                if n is not None:
                    sp.wait_ge(yg_stored[k], 32 * n)
                    sp.sem_inc(own_waits, 1)
                row = sp.value_load(table[0:1, 1, bass.ds(j, 1)], min_val=0, max_val=EXPERTS * REGION)
                sp.dma_start(xg[:, k], gathered[bass.ds(row, GT)].rearrange("(s p) r -> p s r", p=P)
                             ).then_inc(xg_loaded[k], 16)

            for k in range(NG):
                load_tile(k, k, None)
            with sp.Fori(1, ROUNDS) as n:
                for k in range(NG):
                    load_tile(NG * n + k, k, n)
            for k in range(REST):
                load_tile(NG * ROUNDS + k, k, ROUNDS)

            for k in range(NG):
                sp.wait_ge(yg_stored[k], 32 * (ROUNDS + (k < REST)))
            rv = results.rearrange("(k a t p) d -> a p k t d", k=2, a=PAIRS, p=P)
            for a in range(PAIRS):
                for c in range(2):
                    sp.dma_start(yk[:, a, c], rv[a, :, c]).then_inc(yk_loaded[a], 16)
            for a in range(PAIRS):
                sp.wait_ge(combined, a + 1)
                sp.dma_start(ov[:, a], Xo[:, a]).then_inc(stored, 16)
            sp.wait_ge(stored, 16 * PAIRS)

        @block.gpsimd
        def _(pool):
            g = nc.gpsimd
            built = [0]

            def then(ins):
                built[0] += 1
                ins.then_inc(masks, 1)
                pool.wait_ge(masks, built[0])

            then(g.memset(ident[:], 0.0))
            then(g.affine_select(out=ident[:], in_=ident[:], compare_op=ALU.not_equal, fill=1.0, base=0,
                                 pattern=[[-1, P]], channel_multiplier=1))
            then(g.memset(eps[:], EPS))
            then(g.memset(zero[:], 0.0))
            then(g.memset(stripe[:], 1.0))
            then(g.affine_select(out=stripe[:], in_=stripe[:], compare_op=ALU.is_ge, fill=0.0, base=0,
                                 pattern=[[-DK, 2], [-2 * DK, 2 * QUARTER]], channel_multiplier=1))
            then(g.affine_select(out=stripe[:], in_=stripe[:], compare_op=ALU.is_ge, fill=0.0, base=DK - 1,
                                 pattern=[[DK, 2], [2 * DK, 2 * QUARTER]], channel_multiplier=-1))
            then(g.memset(wo[64:128, 0, :, :], 0.0))
            then(g.memset(wo[0:64, 1, :, :], 0.0))
            then(g.memset(negI[:], 0.0))
            assert built[0] == BASICS, built
            then(g.affine_select(out=negI[:], in_=negI[:], compare_op=ALU.not_equal, fill=-1.0, base=0,
                                 pattern=[[-1, P]], channel_multiplier=1))
            for i, value in enumerate((1.5, 1.0)):
                then(g.memset(consts[:, i], value))
            for j in range(2):
                then(g.memset(vPad[j][:], 0.0))
            then(g.memset(consts[:, 2], W_SCALE))
            then(g.iota(iota8[:], [[-1, EXPERTS]], base=EXPERTS, channel_multiplier=0,
                        allow_small_or_imprecise_dtypes=True))
            then(g.memset(ident16[:], 0.0))
            then(g.affine_select(out=ident16[:], in_=ident16[:], compare_op=ALU.not_equal, fill=1.0, base=0,
                                 pattern=[[-1, P]], channel_multiplier=1))
            then(g.memset(ones16[:], 1.0))
            then(g.affine_select(out=before[:], in_=ones16[:], compare_op=ALU.is_gt, fill=0.0, base=0,
                                 pattern=[[1, P]], channel_multiplier=-1))
            then(g.memset(newrow[:], 1.0))
            then(g.memset(newrow[:, :, 0:1], 0.0))
            then(g.iota(region[:], [[REGION, EXPERTS], [0, TILES]], base=0, channel_multiplier=0,
                        allow_small_or_imprecise_dtypes=True))
            then(g.iota(tile_no[:], [[1, MAX_TILES], [0, EXPERTS]], base=0, channel_multiplier=0,
                        allow_small_or_imprecise_dtypes=True))
            then(g.iota(token[:], [[B * S, 2], [P, TILES]], base=0, channel_multiplier=1))
            assert built[0] == BUILT, built

            pool.wait_ge(wfc_loaded, 16)
            pool.sem_inc(own_waits, 1)
            with pool.Fori(0, NE) as e:
                g.tensor_tensor(wfcH[:, e], wfc_f32[:, e], consts[:, 2, 0:1].broadcast_to([P, F]),
                                ALU.mult).then_inc(wfcH_ready, 1)

            pool.wait_ge(wproj_loaded, 48)
            pool.sem_inc(own_waits, 1)
            for part, (lo, hi) in zip(proj_f32, PROJ_PARTS):
                with pool.Fori(0, hi - lo) as e:
                    g.tensor_tensor(wprojH[:, lo + e], part[:, e], consts[:, 2, 0:1].broadcast_to([P, F]),
                                    ALU.mult).then_inc(projH_ready, 1)

            def normalise(k, u):
                pool.wait_ge(rz_ready, u + 1)
                for half in range(2):
                    heads = E[:, k, half * HH:half * HH + HH]
                    g.tensor_tensor(heads, heads, rZ[:, k % 2, :].unsqueeze(1).broadcast_to([P, HH, P]),
                                    ALU.mult).then_inc(attn_ready, 1)

            def inverse_deviation(n):
                pool.wait_ge(seed_ready, n + 1)
                y, z = rstd2[:], newton[:]
                ops = [(z, y, y, ALU.mult), (z, z, half_var[:], ALU.mult), (z, z, consts[:, 0], ALU.add),
                       (y, y, z, ALU.mult)] * 3
                ops += [(rstd2p1[:], y, consts[:, 1], ALU.add), (shift2[:], y, neg_mean[:], ALU.mult)]
                for i, (o, a, b, op) in enumerate(ops):
                    if i == len(ops) - 2 and n:
                        pool.wait_ge(x2_added, 2 * n)
                    ins = g.tensor_tensor(o, a, b, op)
                    if i < len(ops) - 1:
                        ins.then_inc(newton_step, 1)
                        pool.wait_ge(newton_step, n * (len(ops) - 1) + i + 1)
                    else:
                        ins.then_inc(rstd2_ready, 1)

            def ffn_inputs(pair, j):
                tiles = bass.ds(pair * TP, TP)
                pool.wait_ge(hi_ready, pair + 1)
                g.tensor_tensor(xs[:, tiles, D:2 * D], xn[:, j], xs[:, tiles, 0:D], ALU.subtract
                                ).then_inc(lo_ready, 1)

            def four_units(n):
                normalise(0, 4 * n)
                if n > 1:
                    ffn_inputs(2 * n - 3, 1)
                normalise(1, 4 * n + 1)
                if n:
                    inverse_deviation(n - 1)
                normalise(2, 4 * n + 2)
                normalise(3, 4 * n + 3)
                if 0 < n < PAIRS // 2 - 1:
                    ffn_inputs(2 * n - 2, 0)

            for n in range(PAIRS // 2):
                four_units(n)

            def add_norm(pair, j):
                xv = X[:, pair].rearrange("p b c d -> p (b c) d")
                g.tensor_tensor(xv, xv, xn[:, j], ALU.add).then_inc(late_added, 1)

            for j in range(2):
                pool.wait_ge(hi_ready, LATE + j + 1)
                add_norm(LATE + j, j)
            pool.wait_ge(raw_ready, UNITS)
            g.memset(padding, 0.0).then_inc(padding_ready, 1)
            pool.wait_ge(padding_ready, 1)
            g.iota(padding[:, :, 2 * D:ROW].bitcast(I32), [[0, 2], [0, 1]], base=SKIP, channel_multiplier=0
                   ).then_inc(padding_ready, 1)

            for portion, (lo, hi) in enumerate(PORTIONS):
                for k in range(2):
                    if k == 0:
                        pool.wait_ge(slot_ready, portion + 1)
                    else:
                        if portion:
                            for j in range(2):
                                pool.wait_ge(late_ready, 3 + j)
                                add_norm(PAIRS - 2 + j, j)
                        pool.wait_ge(token2_ready, portion + 1)
                    for i in range(lo, hi):
                        g.indirect_dma_start(
                            out=gathered, out_offset=bass.IndirectOffsetOnAxis(ap=slot[:, k, i:i + 1], axis=0),
                            in_=xs[:, i, :], in_offset=None, bounds_check=EXPERTS * REGION - 1,
                            oob_is_err=False).then_inc(scattered[portion], 16)

            def results_out(i, k):
                pool.wait_ge(yg_ready, i + 1)
                pool.sem_inc(own_waits, 1)
                for h in range(2):
                    g.indirect_dma_start(
                        out=results,
                        out_offset=bass.IndirectOffsetOnAxis(ap=xg[:, k, h, 2 * D:ROW].bitcast(I32), axis=0),
                        in_=yg[:, k, h, :], in_offset=None, bounds_check=2 * B * S - 1,
                        oob_is_err=False).then_inc(yg_stored[k], 16)

            with pool.Fori(0, ROUNDS) as n:
                for k in range(NG):
                    results_out(NG * n + k, k)
            for k in range(REST):
                results_out(NG * ROUNDS + k, k)

        @block.scalar
        def _(act):
            s = nc.scalar
            for half in range(2):
                act.wait_ge(k_ready, half + 1)
                s.activation(ks[:, 0, half], k_ps[half], ACT.Copy).then_inc(khi_ready, 1)
            for i in range(2):
                act.wait_ge(v_ready, i + 1)
                s.activation(V[:, 4 * i:4 * i + 4], v_ps[i], ACT.Copy).then_inc(V_ready, 1)
            act.wait_ge(masks, BASICS)

            def deviation(q, tiles):
                act.wait_ge(mv_ready, q)
                s.activation(sd[:, tiles], mv[:, tiles, 1], ACT.Sqrt, bias=eps[:]).then_inc(sd_ready, 1)

            def first_norm(n, again):
                if again:
                    act.wait_ge(t_ready, 2 * n)
                for i in range(TP):
                    at = bass.ds((2 * n + 1) * TP + i, 1)
                    last = s.activation(xn[:, 1, i], X[:, 2 * n + 1, i // 2, i % 2, :], ACT.Identity,
                                        bias=shift[:, at], scale=rstd[:, at])
                last.then_inc(xn1_ready, 1)

            def copy_xnT(n):
                for j in range(2):
                    act.wait_ge(t_ready, 2 * n + j + 1)
                    s.activation(xnT[:, j], t_ps[j], ACT.Copy).then_inc(xnT_ready, 1)

            def high_q(n, again):
                for j in range(2):
                    act.wait_ge(q_ready, 2 * n + j + 1)
                    if again:
                        act.wait_ge(spread[0], 2 * n + j + 1)
                        act.wait_ge(spread[1], 2 * n + j + 1)
                    s.activation(qs[:, j, 0], q_ps[j], ACT.Copy).then_inc(qhi_ready, 1)

            def spread_q_out(n):
                for j in range(2):
                    act.wait_ge(spread[0], 2 * n + j + 3)
                    s.activation(qRep[:, 2 * n + j].rearrange("p (h g) q -> p g h q", h=2)[:, 0:2],
                                 spread_ps[0].rearrange("p g (h q) -> p g h q", h=2), ACT.Copy
                                 ).then_inc(spread_out[0], 1)

            def pad_k(j, pair):
                for b in range(2):
                    for odd in range(2):
                        heads = kPad[:, j].rearrange("p (g o) b s -> p o b g s", o=2)[:, odd, b]
                        last = s.activation(heads, kRep[:, :, pair], ACT.Identity, bias=zero[:],
                                            scale=head_mask[:, b, odd:odd + 1])
                last.then_inc(kPad_ready, 1)

            def spread_v(j, pair):
                for b in range(2):
                    r = slice(64 * b, 64 * b + 64)
                    dst = vPad[j][r].rearrange("p a (h s) -> p a h s", s=P + DK)[:, :, :, 64 * b:64 * b + DK]
                    src = V[r, pair, :].rearrange("p (a h d) -> p a h d", a=2, d=DK)
                    last = s.activation(dst, src, ACT.Copy)
                last.then_inc(vPad_ready, 1)

            deviation(1, slice(0, 2 * TP))
            act.wait_ge(rstd_ready, 1)
            first_norm(0, False)

            def spread_k_out(half):
                act.wait_ge(spread[0], half + 1)
                s.activation(kRep[:, half * QUARTER:half * QUARTER + 2].rearrange("p g a s -> p g (a s)"),
                             spread_ps[0], ACT.Copy).then_inc(spread_out[0], 1)

            spread_k_out(0)
            copy_xnT(0)
            spread_k_out(1)
            high_q(0, False)
            act.wait_ge(mask_ready, 1)
            act.wait_ge(spread_out[0], 2)
            act.wait_ge(spread_out[1], 2)
            pad_k(0, 0)
            deviation(4, slice(2 * TP, TILES))
            act.wait_ge(rstd_ready, 2)
            first_norm(1, True)
            pad_k(1, 1)
            act.wait_ge(masks, BUILT)
            act.wait_ge(V_ready, 2)
            spread_v(0, 0)
            spread_v(1, 1)
            with act.Fori(1, PAIRS // 2 - 1) as n:
                copy_xnT(n)
                spread_q_out(n - 1)
                first_norm(n + 1, True)
                high_q(n, True)
            copy_xnT(PAIRS // 2 - 1)
            spread_q_out(PAIRS // 2 - 2)
            high_q(PAIRS // 2 - 1, True)
            spread_q_out(PAIRS // 2 - 1)

            def copy_o(u, k):
                act.wait_ge(o_ready, u + 1)
                s.activation(oT[:, k % 2], o_ps[:, 0:2 * P], ACT.Copy).then_inc(oT_ready, 1)

            def exps(u, k, again):
                act.wait_ge(s_ready, u + 1)
                if again:
                    act.wait_ge(o_ready, u - 3)
                for i in range(2):
                    s.activation(E[:, k, 8 * i:8 * i + 8], scores[:, 2 * i:2 * i + 2], ACT.Exp,
                                 scale=DK ** -0.5).then_inc(exp_done, 1)

            act.wait_ge(wfcL_ready, NE)
            act.wait_ge(projL_ready, NE)

            def second_norm(n, j, again):
                pair = 2 * n + j
                act.wait_ge(rstd2_ready, n + 1)
                if again:
                    act.wait_ge(lo_ready, pair - 1)
                for i in range(TP):
                    at = slice(j * TP + i, j * TP + i + 1)
                    last = s.activation(xn[:, j, i], X[:, pair, i // 2, i % 2, :], ACT.Identity,
                                        bias=shift2[:, at], scale=rstd2[:, at])
                last.then_inc(xn2_ready, 1)
                act.wait_ge(xn2_ready, pair + 1)
                s.activation(xs[:, bass.ds(pair * TP, TP), 0:D], xn[:, j], ACT.Copy).then_inc(hi_ready, 1)

            def add_norm(n, j):
                pair = 2 * n + j
                act.wait_ge(xn2_ready, pair + 1)
                for i in range(TP):
                    xv = X[:, pair, i // 2, i % 2, :]
                    at = slice(j * TP + i, j * TP + i + 1)
                    last = s.activation(xv, xv, ACT.Identity, bias=shift2[:, at], scale=rstd2p1[:, at])
                last.then_inc(x2_added, 1)

            def copy_x2(pair):
                act.wait_ge(t2_ready, pair + 1)
                s.activation(x2[:, :, bass.ds(pair * BANK, BANK)], t2_ps, ACT.Copy).then_inc(x2_ready, 1)

            def four_units(n, first=False, second=False, third=False, last=False):
                for k in range(4):
                    u = 4 * n + k
                    exps(u, k, not first)
                    if not (first and k < 2):
                        if not first:
                            act.wait_ge(y_ready, u - 3)
                        copy_o(u - 2, k)
                    if k == 0 and not (first or second):
                        second_norm(n - 2, 1, not third)
                    if k == 0 and not first:
                        pad_k(1, 2 * n + 1)
                    if k == 1 and not first:
                        spread_v(1, 2 * n + 1)
                    if k in (1, 2) and not (first or second):
                        add_norm(n - 2, k - 1)
                        copy_x2(2 * n - 5 + k)
                    if k == 2 and not last:
                        pad_k(0, 2 * n + 2)
                    if k == 3 and not last:
                        spread_v(0, 2 * n + 2)
                if not first:
                    second_norm(n - 1, 0, not second)

            four_units(0, first=True)
            four_units(1, second=True)
            four_units(2, third=True)
            four_units(3, last=True)
            second_norm(PAIRS // 2 - 2, 1, True)

            def gelus(i, e, again, x2_pair=None):
                if again:
                    act.wait_ge(dn_ready, i - 1)
                for c in range(FC):
                    if c == FC - 1 and x2_pair:
                        copy_x2(x2_pair)
                    act.wait_ge(up_ready, i * FC + c + 1)
                    if again or e:
                        act.wait_ge(hlo_ready, i * FC + c - 3)
                    s.activation(hid[:, c], up_ps[c], ACT.Gelu, scale=1.0 / W_SCALE).then_inc(h32_ready, 1)
                    s.activation(hidH[:, e, c], up_ps[c], ACT.Gelu, scale=1.0 / W_SCALE).then_inc(h_ready, 1)

            def sigmoid_exps(portion):
                lo, hi = PORTIONS[portion]
                act.wait_ge(rneed, 2 * portion + 2)
                s.activation(rt[:, 1:3, lo:hi], rt[:, 1:3, lo:hi], ACT.Exp, scale=-1.0).then_inc(rexp, 1)

            act.wait_ge(y_ready, UNITS - 3)
            copy_o(UNITS - 2, 0)
            for pair in (LATE, LATE + 1):
                copy_x2(pair)
            sigmoid_exps(0)
            act.wait_ge(y_ready, UNITS - 2)
            copy_o(UNITS - 1, 1)
            for i in range(2):
                gelus(i, i, False)
            for i in range(2):
                gelus(2 + i, i, True, x2_pair=PAIRS - 2 + i)
            gelus(4, 0, True)
            sigmoid_exps(1)
            gelus(5, 1, True)
            with act.Fori(3, PAIRS - 1) as n:
                for e in range(2):
                    gelus(2 * n + e, e, True)
            act.wait_ge(rneed, 6)
            s.activation(r1[:, 4:6], r1[:, 4:6], ACT.Exp).then_inc(rexp, 1)
            for e in range(2):
                gelus(SHARED * (PAIRS - 1) + e, e, True)

            def routed_gelus(i, j, again):
                if again:
                    act.wait_ge(gdn_ready, i - 1)
                for c in range(2):
                    act.wait_ge(gup_ready, 2 * i + c + 1)
                    if again:
                        act.wait_ge(ghlo_ready, 2 * i + c - 3)
                    s.activation(hid[:, 2 * j + c], up_ps[2 * j + c], ACT.Gelu, scale=1.0 / W_SCALE
                                 ).then_inc(gh32_ready, 1)
                    s.activation(gH[:, j, 2 * c:2 * c + 2], up_ps[2 * j + c].rearrange("p (c q) -> p c q", c=2),
                                 ACT.Gelu, scale=1.0 / W_SCALE).then_inc(gh_ready, 1)

            act.wait_ge(dn_ready, SHARED * PAIRS)
            act.wait_ge(hlo_ready, SHARED * PAIRS * FC)
            for j in range(2):
                routed_gelus(j, j, False)
            with act.Fori(1, MAX_TILES // 2) as n:
                for j in range(2):
                    routed_gelus(2 * n + j, j, True)
            if MAX_TILES % 2:
                routed_gelus(MAX_TILES - 1, 0, True)
            act.wait_ge(gate_ready, 2)
            for a in range(PAIRS):
                act.wait_ge(yk_loaded[a], 32)
                for i in range(TP):
                    y = yk[:, a, 1, i]
                    last = s.activation(y, y, ACT.Identity, bias=zero[:],
                                        scale=gate[:, 1, a * TP + i:a * TP + i + 1])
                last.then_inc(gated, 1)

        @block.vector
        def _(dve):
            v = nc.vector

            v.memset(select, 0.0).then_inc(select_ready, 1)
            dve.wait_ge(select_ready, 1)
            dve.wait_ge(masks, BASICS)
            groups = ident[:].rearrange("p (b g x) -> p g b x", b=2, x=16)
            for which in range(2):
                for low in range(2):
                    m = select[:, which, low].rearrange("p g (b r s x) -> p g b r s x", b=2, r=2, s=2)
                    for i in range(2):
                        last = v.tensor_copy(m[:, :, :, i, low] if which == 0 else m[:, :, :, low, i], groups)
            last.then_inc(select_ready, 1)
            v.tensor_reduce(head_mask[:], stripe[:].rearrange("p o (b j) -> p b o j", b=2), AX_X, ALU.add
                            ).then_inc(mask_ready, 1)
            for half in range(2):
                dve.wait_ge(khi_ready, half + 1)
                v.tensor_tensor(ks[:, 1, half], k_ps[half], ks[:, 0, half], ALU.subtract).then_inc(klo_ready, 1)

            def first_stats(q):
                dve.wait_ge(x_loaded[q], 16)
                own = range(8 * q, 8 * q + 8)
                for i in own:
                    last = v.bn_stats(stats1[:, i, :], X[:, i // 4, i // 2 % 2, i % 2, :])
                last.then_inc(ln_step, 1)
                dve.wait_ge(ln_step, q + 1)
                for i in own:
                    last = v.bn_aggr(mv[:, i, :], stats1[:, i, :])
                last.then_inc(mv_ready, 1)

            def inverse(i, tiles):
                dve.wait_ge(sd_ready, i + 1)
                v.reciprocal(rstd[:, tiles], sd[:, tiles]).then_inc(inv_step, 1)
                dve.wait_ge(inv_step, i + 1)
                v.scalar_tensor_tensor(shift[:, tiles], mv[:, tiles, 0], -1.0, rstd[:, tiles], ALU.mult, ALU.mult
                                       ).then_inc(rstd_ready, 1)

            def first_norm(n, again):
                if again:
                    dve.wait_ge(t_ready, 2 * n - 1)
                for i in range(TP):
                    at = (2 * n) * TP + i
                    last = v.tensor_scalar(xn[:, 0, i], X[:, 2 * n, i // 2, i % 2, :], mv[:, bass.ds(at, 1), 0],
                                           rstd[:, bass.ds(at, 1)], ALU.subtract, ALU.mult)
                last.then_inc(xn_ready, 1)

            def low_q(n):
                for j in range(2):
                    dve.wait_ge(qhi_ready, 2 * n + j + 1)
                    v.tensor_tensor(qs[:, j, 1], q_ps[j], qs[:, j, 0], ALU.subtract).then_inc(qlo_ready, 1)

            def spread_q_out(n):
                for j in range(2):
                    dve.wait_ge(spread[1], 2 * n + j + 3)
                    v.tensor_copy(qRep[:, 2 * n + j].rearrange("p (h g) q -> p g h q", h=2)[:, 2:4],
                                  spread_ps[1].rearrange("p g (h q) -> p g h q", h=2)).then_inc(spread_out[1], 1)

            first_stats(0)
            inverse(0, slice(0, 2 * TP))
            first_norm(0, False)

            def spread_k_out(half):
                dve.wait_ge(spread[1], half + 1)
                v.tensor_copy(kRep[:, half * QUARTER + 2:half * QUARTER + 4].rearrange("p g a s -> p g (a s)"),
                              spread_ps[1]).then_inc(spread_out[1], 1)

            def low_w(e):
                dve.wait_ge(wfcH_ready, e + 1)
                v.scalar_tensor_tensor(wfcL[:, e], wfc_f32[:, e], W_SCALE, wfcH[:, e],
                                       ALU.mult, ALU.subtract).then_inc(wfcL_ready, 1)

            def low_proj(part, e):
                lo = PROJ_PARTS[part][0]
                dve.wait_ge(projH_ready, lo + e + 1)
                v.scalar_tensor_tensor(wprojL[:, lo + e], proj_f32[part][:, e], W_SCALE, wprojH[:, lo + e],
                                       ALU.mult, ALU.subtract).then_inc(projL_ready, 1)

            first_stats(1)
            spread_k_out(0)
            first_stats(2)
            spread_k_out(1)
            first_stats(3)
            low_q(0)
            inverse(1, slice(2 * TP, TILES))
            first_norm(1, True)
            with dve.Fori(1, PAIRS // 2 - 1) as n:
                spread_q_out(n - 1)
                first_norm(n + 1, True)
                for i in range(4):
                    low_w(4 * n - 4 + i)
                low_q(n)
                for i in range(2):
                    low_proj(0, 2 * n - 2 + i)
            spread_q_out(PAIRS // 2 - 2)
            for e in range(8, NE):
                low_w(e)
            low_q(PAIRS // 2 - 1)
            for i in range(3):
                low_proj(1, i)
            spread_q_out(PAIRS // 2 - 1)
            for i in range(3, 5):
                low_proj(1, i)
            low_proj(2, 0)

            def pair_stats(n, j):
                step = LN2_STEPS * n + 2 * j
                own = range(j * TP, j * TP + TP)
                dve.wait_ge(x_added, 4 * n + 2 * j + 2)
                for i in own:
                    last = v.bn_stats(stats[:, i, :], X[:, 2 * n + j, i // 2 % 2, i % 2, :])
                last.then_inc(ln2_step, 1)
                dve.wait_ge(ln2_step, step + 1)
                dve.sem_inc(own_waits, 1)
                for i in own:
                    last = v.bn_aggr(mv2[:, i, :], stats[:, i, :])
                last.then_inc(ln2_step, 1)

            def deviation_seed(n, again):
                if again:
                    dve.wait_ge(xn2_ready, 2 * n)
                    dve.sem_inc(own_waits, 1)
                dve.wait_ge(ln2_step, LN2_STEPS * n + 4)
                v.tensor_scalar(var2[:], mv2[:, :, 1], EPS, None, ALU.add).then_inc(ln2_step, 1)
                dve.wait_ge(ln2_step, LN2_STEPS * n + 5)
                v.tensor_scalar(half_var[:], var2[:], -0.5, None, ALU.mult)
                v.tensor_scalar(neg_mean[:], mv2[:, :, 0], -1.0, None, ALU.mult)
                v.tensor_scalar(rstd2[:].bitcast(I32), var2[:].bitcast(I32), -0.5, float(0x5f3759df),
                                ALU.mult, ALU.add).then_inc(seed_ready, 1)

            def max_heads(u, k):
                dve.wait_ge(raw_ready, u + 1)
                v.tensor_reduce(Mx[:, k % 2, :], scores.rearrange("p b (h q) -> p q (b h)", q=P),
                                AX_X, ALU.max).then_inc(max_ready, 1)

            def sum_heads(u, k):
                dve.wait_ge(exp_done, 2 * u + 2)
                v.tensor_reduce(Z[:, k % 2, :], E[:, k].rearrange("p h q -> p q h"), AX_X,
                                ALU.add).then_inc(z_ready, 1)
                dve.wait_ge(z_ready, u + 1)
                v.reciprocal(rZ[:, k % 2, :], Z[:, k % 2, :]).then_inc(rz_ready, 1)

            def add_attention(u, qh, pair):
                dve.wait_ge(y_ready, u + 1)
                v.tensor_tensor(X[:, pair, :, qh, :], X[:, pair, :, qh, :],
                                y_ps[:, 0:2 * D].rearrange("p (b d) -> p b d", b=2), ALU.add).then_inc(x_added, 1)

            def four_units(n, first, second):
                for k in range(4):
                    u = 4 * n + k
                    max_heads(u, k)
                    if not (first and k == 0):
                        if not (first and k < 3):
                            dve.wait_ge(attn_ready, 2 * u - 4)
                        sum_heads(u - 1, (k - 1) % 4)
                    if not (first and k < 3):
                        add_attention(u - 3, (k + 1) % 2, 2 * n + (k - 3) // 2)
                    if k in (1, 2) and not first:
                        pair_stats(n - 1, k - 1)
                    if k == 2 and not first:
                        deviation_seed(n - 1, not second)

            four_units(0, True, False)
            four_units(1, False, True)
            with dve.Fori(2, PAIRS // 2) as n:
                four_units(n, False, False)
            dve.wait_ge(attn_ready, 2 * UNITS - 4)
            sum_heads(UNITS - 1, 3)
            dve.wait_ge(small_loaded, 32)
            v.tensor_copy(centH[:], cent[:]).then_inc(rstep, 1)
            dve.wait_ge(rstep, 1)
            v.tensor_tensor(centL[:], cent[:], centH[:], ALU.subtract).then_inc(rstep, 1)

            def late_low(pair, j):
                tiles = slice(pair * TP, pair * TP + TP)
                v.tensor_tensor(xs[:, tiles, D:2 * D], xn[:, j], xs[:, tiles, 0:D], ALU.subtract
                                ).then_inc(late_ready, 1)

            add_attention(UNITS - 3, 1, PAIRS - 2)
            for j in range(2):
                dve.wait_ge(hi_ready, LATE + j + 1)
                late_low(LATE + j, j)
            add_attention(UNITS - 2, 0, PAIRS - 1)

            def add_shared(pair, j):
                if pair < LATE:
                    dve.wait_ge(x2_added, pair + 1)
                else:
                    dve.wait_ge(late_added, pair - LATE + 1)
                dve.wait_ge(dn_ready, SHARED * pair + SHARED)
                xv = X[:, pair].rearrange("p b c d -> p (b c d)")
                v.scalar_tensor_tensor(xv, dn_ps[j], 1.0 / W_SCALE, xv, ALU.mult, ALU.add).then_inc(acc_done, 1)

            def low_hidden(i, c):
                dve.wait_ge(h_ready, i * FC + c + 1)
                dve.wait_ge(h32_ready, i * FC + c + 1)
                if i > 1:
                    dve.wait_ge(dn_ready, i - 1)
                v.tensor_tensor(hidL[:, i % 2, c], hid[:, c], hidH[:, i % 2, c], ALU.subtract
                                ).then_inc(hlo_ready, 1)

            steps = [2]

            def then(ins):
                steps[0] += 1
                ins.then_inc(rstep, 1)
                dve.wait_ge(rstep, steps[0])

            cum, tot = (rt[:, i].rearrange("p t e -> p (t e)").rearrange("p (e t) -> p e t", e=EXPERTS)
                        for i in (10, 11))

            def scores_in(portion):
                lo, hi = PORTIONS[portion]
                t, tok8 = slice(lo, hi), [P, hi - lo, EXPERTS]
                dve.wait_ge(route_ready, portion + 1)
                raw = r_ps[:, 0:(hi - lo) * EXPERTS].rearrange("p (t e) -> p t e", e=EXPERTS)
                then(v.tensor_copy(rt[:, 0, t], raw))
                v.tensor_copy(rt[:, 1, t], rt[:, 0, t]).then_inc(rneed, 1)
                v.tensor_tensor(rt[:, 2, t], rt[:, 0, t], bias8[:].unsqueeze(1).broadcast_to(tok8), ALU.add
                                ).then_inc(rneed, 1)

            def choose(portion, i=None):
                def low(c):
                    if i is not None:
                        low_hidden(i, c)

                lo, hi = PORTIONS[portion]
                t, tok8 = slice(lo, hi), [P, hi - lo, EXPERTS]

                def all8(x):
                    return x.unsqueeze(2).broadcast_to(tok8)

                def pick(scores_, slot, k):
                    then(v.tensor_reduce(r1[:, k, t], scores_, AX_X, ALU.max))
                    then(v.tensor_tensor(rt[:, slot, t], scores_, all8(r1[:, k, t]), ALU.is_equal))
                    then(v.tensor_tensor(rt[:, slot, t], rt[:, slot, t], iota8[:].unsqueeze(1).broadcast_to(tok8),
                                         ALU.mult))
                    then(v.tensor_reduce(r1[:, k + 1, t], rt[:, slot, t], AX_X, ALU.max))
                    then(v.tensor_tensor(rt[:, slot + 1, t], rt[:, slot, t], all8(r1[:, k + 1, t]), ALU.is_equal))

                dve.wait_ge(rexp, portion + 1)
                then(v.tensor_scalar(rt[:, 1:3, t], rt[:, 1:3, t], 1.0, None, ALU.add))
                then(v.reciprocal(rt[:, 3:5, t], rt[:, 1:3, t]))
                pick(rt[:, 4, t], 5, 0)
                low(0)
                then(v.scalar_tensor_tensor(rt[:, 7, t], rt[:, 6, t], -4.0, rt[:, 4, t], ALU.mult, ALU.add))
                pick(rt[:, 7, t], 8, 2)
                low(1)
                v.tensor_tensor(member[:, :, t].rearrange("p e t -> p t e"), rt[:, 6, t], rt[:, 9, t], ALU.add
                                ).then_inc(member_ready, 1)
                low(2)
                low(3)

            def place(portion, i):
                lo, hi = PORTIONS[portion]
                t = slice(lo, hi)
                dve.wait_ge(rank_ready, portion + 1)
                then(v.tensor_copy(tot[:, :, t], tot_ps[:, :, 0:hi - lo]))
                then(v.tensor_tensor_scan(rt[:, 10].rearrange("p t e -> p (t e)"),
                                          newrow[:].rearrange("p e t -> p (e t)"),
                                          rt[:, 11].rearrange("p t e -> p (t e)"), 0.0, ALU.mult, ALU.add))
                if hi == TILES:
                    then(v.tensor_copy(counts[:], cum[:, :, TILES - 1]))
                c = cum[:, :, t]
                then(v.tensor_tensor(c, c, tot[:, :, t], ALU.subtract))
                then(v.tensor_tensor(c, c, rank_ps[:, :, 0:hi - lo], ALU.add))
                then(v.tensor_tensor(c, c, region[:, :, t], ALU.add))
                low_hidden(i, 0)
                for k, hot in enumerate((6, 9)):
                    then(v.tensor_tensor(rt[:, 5, t], rt[:, hot, t], c.rearrange("p e t -> p t e"), ALU.mult))
                    then(v.tensor_reduce(r1[:, 9, t], rt[:, 5, t], AX_X, ALU.add))
                    then(v.tensor_copy(slot[:, k, t], r1[:, 9, t]))
                    low_hidden(i, k + 1)
                v.tensor_copy(xs[:, t, 2 * D:ROW].bitcast(I32), token[:, 0, t].unsqueeze(2)).then_inc(slot_ready, 1)
                low_hidden(i, 3)

            def low_expert(i):
                for c in range(FC):
                    low_hidden(i, c)
                    if c == 1 and i % 2 == 0:
                        add_shared(i // 2 - 1, (i // 2 - 1) % 2)

            def second_rows(portion):
                lo, hi = PORTIONS[portion]
                dve.wait_ge(scattered[portion], 16 * (hi - lo))
                v.tensor_copy(xs[:, lo:hi, 2 * D:ROW].bitcast(I32), token[:, 1, lo:hi].unsqueeze(2)
                              ).then_inc(token2_ready, 1)

            dve.wait_ge(route_ready, 1)
            then(v.memset(rt[:, 11], 0.0))
            scores_in(0)
            choose(0)
            add_attention(UNITS - 1, 1, PAIRS - 1)
            place(0, 0)

            dve.wait_ge(x_added, UNITS)
            dve.sem_inc(own_waits, 1)
            dve.wait_ge(xn2_ready, LATE + 2)
            for i in range(2 * TP):
                last = v.bn_stats(stats[:, i, :], X[:, PAIRS - 2 + i // TP, i // 2 % 2, i % 2, :])
            then(last)
            for i in range(2 * TP):
                last = v.bn_aggr(mv2[:, i, :], stats[:, i, :])
            then(last)
            low_hidden(1, 0)
            low_hidden(1, 1)
            y, z = rstd2[:], newton[:]
            then(v.tensor_scalar(var2[:], mv2[:, :, 1], EPS, None, ALU.add))
            low_hidden(1, 2)
            then(v.tensor_scalar(y.bitcast(I32), var2[:].bitcast(I32), -0.5, float(0x5f3759df), ALU.mult, ALU.add))
            for _ in range(3):
                then(v.scalar_tensor_tensor(z, y, -0.5, y, ALU.mult, ALU.mult))
                then(v.scalar_tensor_tensor(z, z, 1.0, var2[:], ALU.mult, ALU.mult))
                then(v.scalar_tensor_tensor(y, z, 1.5, y, ALU.add, ALU.mult))
            dve.wait_ge(late_added, 2)
            for j in range(2):
                pair = PAIRS - 2 + j
                for i in range(TP):
                    at = j * TP + i
                    last = v.tensor_scalar(xn[:, j, i], X[:, pair, i // 2, i % 2, :], mv2[:, at, 0:1],
                                           y[:, at:at + 1], ALU.subtract, ALU.mult)
                then(last)
                then(v.tensor_copy(xs[:, pair * TP:pair * TP + TP, 0:D], xn[:, j]))
                late_low(pair, j)
                if j == 0:
                    low_hidden(1, 3)
            low_expert(2)
            low_expert(3)
            scores_in(1)
            low_expert(4)
            choose(1, 5)
            second_rows(0)
            low_expert(6)
            place(1, 7)
            dve.wait_ge(slot_ready, 2)

            then(v.tensor_copy(r1[:, 9, 0:EXPERTS], counts[:]))
            nt, end = r1[:, 10, 0:EXPERTS], r1[:, 11, 0:EXPERTS]
            then(v.tensor_scalar(tiles_of[:], r1[:, 9, 0:EXPERTS], float(GT - 1), None, ALU.add))
            then(v.tensor_scalar(tiles_of[:], tiles_of[:], GT.bit_length() - 1, None, ALU.logical_shift_right))
            low_hidden(8, 0)
            then(v.tensor_copy(nt, tiles_of[:]))
            then(v.tensor_copy(end, nt))
            for e in range(1, EXPERTS):
                then(v.tensor_tensor(end[:, e:e + 1], end[:, e - 1:e], nt[:, e:e + 1], ALU.add))
            low_hidden(8, 1)
            add_shared(3, 1)
            wide = [P, MAX_TILES, EXPERTS]
            passed = rt[:, 0:2].rearrange("p a t e -> p (a t e)")[:, 0:MAX_TILES * EXPERTS].rearrange(
                "p (j e) -> p j e", e=EXPERTS)
            spent = rt[:, 8:10].rearrange("p a t e -> p (a t e)")[:, 0:MAX_TILES * EXPERTS].rearrange(
                "p (j e) -> p j e", e=EXPERTS)
            tj = rt[:, 7].rearrange("p t e -> p (t e)")
            ej, sj, rj = (tj[:, i * MAX_TILES:(i + 1) * MAX_TILES] for i in range(3))

            for n, hot in enumerate((6, 9)):
                then(v.tensor_tensor(rt[:, 5], rt[:, hot], rt[:, 3], ALU.mult))
                then(v.tensor_reduce(r1[:, 4 + n], rt[:, 5], AX_X, ALU.add))
            low_hidden(8, 2)
            then(v.tensor_tensor(passed, tile_no[:], end.unsqueeze(1).broadcast_to(wide), ALU.is_ge))
            then(v.tensor_tensor(spent, passed, nt.unsqueeze(1).broadcast_to(wide), ALU.mult))
            then(v.tensor_reduce(ej, passed, AX_X, ALU.add))
            then(v.tensor_reduce(sj, spent, AX_X, ALU.add))
            low_hidden(8, 3)
            then(v.tensor_tensor(rj, tile_no[:, :, 0], sj, ALU.subtract))
            then(v.tensor_scalar(rj, rj, float(GT), None, ALU.mult))
            then(v.scalar_tensor_tensor(rj, ej, float(REGION), rj, ALU.mult, ALU.add))
            then(v.tensor_scalar(table[:, 1], rj, float(EXPERTS * REGION), None, ALU.min))
            v.tensor_scalar(table[:, 0], ej, float(EXPERTS - 1), None, ALU.min).then_inc(table_ready, 1)

            then(v.tensor_tensor(r1[:, 6], r1[:, 4], r1[:, 5], ALU.max))
            v.tensor_tensor(r1[:, 4], r1[:, 4], r1[:, 6], ALU.subtract).then_inc(rneed, 1)
            v.tensor_tensor(r1[:, 5], r1[:, 5], r1[:, 6], ALU.subtract).then_inc(rneed, 1)
            for i in range(9, SHARED * PAIRS):
                low_expert(i)
                if i == 13:
                    second_rows(1)
            add_shared(PAIRS - 1, 1)
            dve.wait_ge(rexp, 3)
            then(v.tensor_tensor(r1[:, 7], r1[:, 4], r1[:, 5], ALU.add))
            then(v.reciprocal(r1[:, 8], r1[:, 7]))
            for n in range(2):
                v.tensor_tensor(gate[:, n], r1[:, 4 + n], r1[:, 8], ALU.mult).then_inc(gate_ready, 1)

            def routed_copies(i, k, again):
                dve.wait_ge(gT_ready, i + 1)
                if again:
                    dve.wait_ge(gup_ready, 2 * i - 2)
                v.tensor_copy(xgT[:, k % 2], g_ps[k % 2]).then_inc(xgT_ready, 1)

            def results_out(i, k):
                dve.wait_ge(gdn_ready, i + 1)
                v.tensor_scalar(yg[:, k].rearrange("p s d -> p (s d)"), dn_ps[k % 2][:, 0:2 * D], 1.0 / W_SCALE, None,
                                ALU.mult).then_inc(yg_ready, 1)

            def routed_lows(i, j):
                for c in range(2):
                    dve.wait_ge(gh_ready, 2 * i + c + 1)
                    dve.wait_ge(gh32_ready, 2 * i + c + 1)
                    v.tensor_tensor(gL[:, j, 2 * c:2 * c + 2], hid[:, 2 * j + c].rearrange("p (c q) -> p c q", c=2),
                                    gH[:, j, 2 * c:2 * c + 2], ALU.subtract).then_inc(ghlo_ready, 1)

            routed_copies(0, 0, False)
            routed_copies(1, 1, False)
            for k in range(NG):
                routed_lows(k, k % 2)
                routed_copies(k + 2, k % 2, True)
                if k:
                    results_out(k - 1, k - 1)
            with dve.Fori(1, ROUNDS) as n:
                for k in range(NG):
                    routed_lows(NG * n + k, k % 2)
                    routed_copies(NG * n + k + 2, k % 2, True)
                    results_out(NG * n + k - 1, (k - 1) % NG)
            for k in range(REST):
                i = NG * ROUNDS + k
                routed_lows(i, k % 2)
                if i + 2 < MAX_TILES:
                    routed_copies(i + 2, k % 2, True)
                results_out(i - 1, (k - 1) % NG)
            results_out(MAX_TILES - 1, REST - 1)

            dve.wait_ge(gate_ready, 2)
            for a in range(PAIRS):
                dve.wait_ge(yk_loaded[a], 32)
                for i in range(TP):
                    xv = X[:, a, i // 2, i % 2, :]
                    last = v.scalar_tensor_tensor(xv, yk[:, a, 0, i], gate[:, 0, a * TP + i:a * TP + i + 1], xv,
                                                  ALU.mult, ALU.add)
                last.then_inc(combined_half, 1)
                dve.wait_ge(combined_half, a + 1)
                dve.wait_ge(gated, a + 1)
                xv = X[:, a].rearrange("p b c d -> p (b c d)")
                v.tensor_tensor(xv, xv, yk[:, a, 1].rearrange("p t d -> p (t d)"), ALU.add).then_inc(combined, 1)

        @block.tensor
        def _(pe):
            t = nc.tensor
            pe.wait_ge(ctx_loaded, 48)
            for half in range(2):
                for b in range(2):
                    last = t.matmul(k_ps[half][64 * b:64 * b + 64, :], wk[:, 64 * half:64 * half + 64],
                                    ctxT[:, :, b], start=True, stop=True)
                last.then_inc(k_ready, 1)
            for i in range(2):
                for p in range(4):
                    last = t.matmul(v_ps[i][:, D * p:D * p + D], ctxT[:, 4 * i + p].rearrange("p b s -> p (b s)"), wv,
                                    start=True, stop=True)
                last.then_inc(v_ready, 1)

            pe.wait_ge(masks, BASICS)
            pe.wait_ge(wq_loaded, 16)

            def transposes(n, again):
                for j in range(2):
                    pe.wait_ge((xn_ready, xn1_ready)[j], n + 1)
                    if again:
                        pe.wait_ge(xnT_ready, 2 * n + j - 1)
                    for i in range(TP):
                        last = t.transpose(t_ps[j][:, P * i:P * i + P], xn[:, j, i, :], ident[:])
                    last.then_inc(t_ready, 1)

            def project_q(n, again):
                for j in range(2):
                    pe.wait_ge(xnT_ready, 2 * n + j + 1)
                    if again:
                        pe.wait_ge(qlo_ready, 2 * n + j - 1)
                    for half in range(2):
                        for b in range(2):
                            last = t.matmul(q_ps[j][64 * b:64 * b + 64, S * half:S * half + S],
                                            wq[:, 64 * half:64 * half + 64], xnT[:, j, S * b:S * b + S],
                                            start=True, stop=True)
                    last.then_inc(q_ready, 1)

            def spread_parts(i, which, high, low, reused):
                for side in range(2):
                    if reused:
                        pe.wait_ge(spread_out[side], i)
                    for g in range(2):
                        sel = 2 * side + g
                        t.matmul(spread_ps[side][:, g, :], select[:, which, 0, sel], high, start=True, stop=False)
                        last = t.matmul(spread_ps[side][:, g, :], select[:, which, 1, sel], low, start=False,
                                        stop=True)
                    last.then_inc(spread[side], 1)

            def spread_q(n):
                for j in range(2):
                    pe.wait_ge(qlo_ready, 2 * n + j + 1)
                    spread_parts(2 * n + j + 2, 1, qs[:, j, 0], qs[:, j, 1], True)

            pe.wait_ge(V_ready, 2)
            pe.wait_ge(select_ready, 2)
            pe.wait_ge(klo_ready, 2)
            spread_parts(0, 0, ks[:, 0, 0], ks[:, 1, 0], False)
            transposes(0, False)
            spread_parts(1, 0, ks[:, 0, 1], ks[:, 1, 1], True)
            project_q(0, False)
            with pe.Fori(1, PAIRS // 2) as n:
                transposes(n, True)
                spread_q(n - 1)
                project_q(n, True)
            spread_q(PAIRS // 2 - 1)
            pe.wait_ge(masks, BUILT)

            def raw_scores(u, k, pair, first):
                for i in range(4):
                    if not first and i % 2 == 0:
                        pe.wait_ge(exp_done, 2 * u + i // 2 - 1)
                    for h in range(4 * i, 4 * i + 4):
                        last = t.matmul(scores[:, i, P * (h % 4):P * (h % 4) + P],
                                        kPad[:, k // 2, h].rearrange("p b s -> p (b s)"),
                                        qRep[:, pair, h // 2, P * (k % 2):P * (k % 2) + P],
                                        start=(h % 4 == 0), stop=False, skip_group_check=True)
                last.then_inc(raw_ready, 1)

            def minus_max(u, k):
                pe.wait_ge(max_ready, u + 1)
                for i in range(4):
                    last = t.matmul(scores[:, i, :], negI[:], Mx[:, k % 2, :].unsqueeze(1).broadcast_to([P, 4, P]),
                                    start=False, stop=True, skip_group_check=True)
                last.then_inc(s_ready, 1)

            def weighted_values(u, k, half):
                pe.wait_ge(attn_ready, 2 * u + half + 1)
                for h in range(HH):
                    last = t.matmul(o_ps[:, P * half:P * half + P], vPad[k // 2][:, half, h * P:(h + 1) * P],
                                    E[:, k, half * HH + h, :], start=(h == 0), stop=(h == HH - 1))
                if half:
                    last.then_inc(o_ready, 1)

            def project_out(u, k, first):
                pe.wait_ge(oT_ready, u + 1)
                if not first:
                    pe.wait_ge(x_added, u)
                for b in range(2):
                    for half in range(2):
                        last = t.matmul(y_ps[:, D * b:D * b + D], oT[:, k % 2, half], wo[:, b, half],
                                        start=(half == 0), stop=(half == 1))
                last.then_inc(y_ready, 1)

            pe.wait_ge(wo_loaded, 64)
            for side in range(2):
                pe.wait_ge(spread_out[side], PAIRS + 2)

            def four_units(n, first=False, inputs=False):
                for k in range(4):
                    u = 4 * n + k
                    if k % 2 == 0:
                        pe.wait_ge(kPad_ready, 2 * n + k // 2 + 1)
                    raw_scores(u, k, 2 * n + k // 2, first and k == 0)
                    if not (first and k < 3):
                        project_out(u - 3, (k - 3) % 4, first and k == 3)
                    values = not (first and k < 2)
                    if values:
                        if k % 2 == 0:
                            pe.wait_ge(vPad_ready, 2 * n + k // 2)
                        if first and k == 3:
                            pe.wait_ge(oT_ready, 1)
                        weighted_values(u - 2, (k - 2) % 4, 0)
                    minus_max(u, k)
                    if values:
                        weighted_values(u - 2, (k - 2) % 4, 1)
                    if k in (1, 2) and inputs:
                        ffn_transposes(2 * n - 5 + k, n > 2 or k > 1)

            def ffn_transposes(pair, again):
                if pair < LATE:
                    pe.wait_ge(lo_ready, pair + 1)
                else:
                    pe.wait_ge(late_ready, pair - LATE + 1)
                if again:
                    pe.wait_ge(x2_ready, pair)
                for l in range(2):
                    for i in range(TP):
                        last = t.matmul(t2_ps[:, l, P * i:P * i + P], xs[:, pair * TP + i, D * l:D * l + D],
                                        ident16[:], start=True, stop=True)
                last.then_inc(t2_ready, 1)

            four_units(0, True)
            four_units(1)
            for n in range(2, PAIRS // 2):
                four_units(n, inputs=True)
            pe.wait_ge(vPad_ready, PAIRS)
            project_out(UNITS - 3, 1, False)
            for half in range(2):
                weighted_values(UNITS - 2, 2, half)

            pe.wait_ge(rstep, 2)
            pe.wait_ge(wfcL_ready, NE)

            def route(portion):
                lo, hi = PORTIONS[portion]
                pe.wait_ge(x2_ready, hi // TP)
                for i in range(lo, hi):
                    tok = slice(P * i, P * i + P)
                    o = r_ps[:, EXPERTS * (i - lo):EXPERTS * (i - lo) + EXPERTS]
                    t.matmul(o, x2[:, 0, tok], centL[:], start=True, stop=False)
                    t.matmul(o, x2[:, 1, tok], centH[:], start=False, stop=False)
                    last = t.matmul(o, x2[:, 0, tok], centH[:], start=False, stop=True)
                last.then_inc(route_ready, 1)

            def ranks(portion):
                lo, hi = PORTIONS[portion]
                pe.wait_ge(member_ready, portion + 1)
                t.matmul(rank_ps[:, :, 0:hi - lo], before[:], member[:, :, lo:hi], start=True, stop=True)
                t.matmul(tot_ps[:, :, 0:hi - lo], ones16[:], member[:, :, lo:hi], start=True, stop=True
                         ).then_inc(rank_ready, 1)

            def shared_up(pair, e, i, c, first=False):
                if not first:
                    pe.wait_ge(h_ready, i * FC + c - 3)
                f = slice(c * P, c * P + P)
                tok = bass.ds(pair * BANK, BANK)
                t.matmul(up_ps[c], wfcH[:, e, f], x2[:, 1, tok], start=True, stop=False)
                t.matmul(up_ps[c], wfcL[:, e, f], x2[:, 0, tok], start=False, stop=False)
                t.matmul(up_ps[c], wfcH[:, e, f], x2[:, 0, tok], start=False, stop=True).then_inc(up_ready, 1)

            def shared_expert(pair, j, e, i, dn_reused=True, first=False, last=False):
                for c in range(FC):
                    if c == 0:
                        shared_up(pair, e, i, FC - 1, first=first)
                    elif not last:
                        shared_up(pair + e, 1 - e, i + 1, c - 1)
                    pe.wait_ge(hlo_ready, i * FC + c + 1)
                    if c == 0 and e == 0 and dn_reused:
                        pe.wait_ge(acc_done, pair - 1)
                    for q in range(TP):
                        o, tok, f = dn_ps[j][:, P * q:P * q + P], slice(P * q, P * q + P), slice(c * D, c * D + D)
                        t.matmul(o, hidH[:, e, c, tok], wprojL[:, e, f], start=(e == 0 and c == 0 and q == 0),
                                 stop=False, skip_group_check=True)
                        t.matmul(o, hidH[:, e, c, tok], wprojH[:, e, f], start=False, stop=False,
                                 skip_group_check=True)
                        last_product = t.matmul(o, hidL[:, e, c, tok], wprojH[:, e, f], start=False,
                                                stop=(e == 1 and c == FC - 1), skip_group_check=True)
                last_product.then_inc(dn_ready, 1)

            for j in range(2):
                ffn_transposes(LATE + j, True)
            project_out(UNITS - 2, 2, False)
            route(0)
            for half in range(2):
                weighted_values(UNITS - 1, 3, half)
            project_out(UNITS - 1, 3, False)
            pe.wait_ge(exp_done, 2 * UNITS)
            for c in range(FC - 1):
                shared_up(0, 0, 0, c, first=True)
            ranks(0)
            pe.wait_ge(projL_ready, NE)
            pe.wait_ge(oT_ready, UNITS)
            shared_expert(0, 0, 0, 0, False, first=True)
            shared_expert(0, 0, 1, 1)
            pe.wait_ge(slot_ready, 1)
            ffn_transposes(PAIRS - 2, True)
            shared_expert(1, 1, 0, 2, False)
            ffn_transposes(PAIRS - 1, True)
            shared_expert(1, 1, 1, 3)
            route(1)
            for e in range(SHARED):
                shared_expert(2, 0, e, 4 + e)
            shared_expert(3, 1, 0, 6)
            ranks(1)
            shared_expert(3, 1, 1, 7)
            with pe.Fori(2, PAIRS // 2 - 1) as n:
                for j in range(2):
                    for e in range(SHARED):
                        shared_expert(2 * n + j, j, e, (2 * n + j) * SHARED + e)
            for j in range(2):
                for e in range(SHARED):
                    pair = PAIRS - 2 + j
                    shared_expert(pair, j, e, pair * SHARED + e, last=(j == 1 and e == 1))

            def gather_transpose(i, k, n, first_two=False):
                pe.wait_ge(xg_loaded[k], 16 * n + 16)
                if not first_two:
                    pe.wait_ge(xgT_ready, i - 1)
                for l in range(2):
                    for h in range(2):
                        last = t.transpose(g_ps[k % 2][:, l, P * h:P * h + P], xg[:, k, h, D * l:D * l + D],
                                           ident16[:])
                last.then_inc(gT_ready, 1)

            def experts_of(i, count):
                _, values = nc.values_load_multi_w_load_instructions(
                    table[0:1, 0, bass.ds(i, count)], engines=[mybir.EngineType.PE], min_val=0, max_val=EXPERTS - 1)
                return [value + SHARED for value in values]

            def routed_up(i, k, e, first):
                j = k % 2
                pe.wait_ge(xgT_ready, i + 1)
                for c in range(FC):
                    if not first and c % 2 == 0:
                        pe.wait_ge(gh_ready, 2 * i + c // 2 - 3)
                    o = up_ps[2 * j + c // 2][:, GT * (c % 2):GT * (c % 2) + GT]
                    f = bass.ds(c * P, P)
                    t.matmul(o, wfcH[:, e, f], xgT[:, j, 1], start=True, stop=False)
                    t.matmul(o, wfcL[:, e, f], xgT[:, j, 0], start=False, stop=False)
                    last = t.matmul(o, wfcH[:, e, f], xgT[:, j, 0], start=False, stop=True)
                    if c % 2:
                        last.then_inc(gup_ready, 1)

            def routed_down(i, k, e, first):
                j = k % 2
                pe.wait_ge(ghlo_ready, 2 * i + 2)
                if not first:
                    pe.wait_ge(yg_ready, i - 1)
                for h in range(2):
                    for c in range(FC):
                        o, tok, f = dn_ps[j][:, P * h:P * h + P], slice(P * h, P * h + P), bass.ds(c * D, D)
                        t.matmul(o, gH[:, j, c, tok], wprojL[:, e, f], start=(c == 0), stop=False)
                        t.matmul(o, gH[:, j, c, tok], wprojH[:, e, f], start=False, stop=False)
                        last = t.matmul(o, gL[:, j, c, tok], wprojH[:, e, f], start=False, stop=(c == FC - 1))
                last.then_inc(gdn_ready, 1)

            pe.wait_ge(table_ready, 1)
            pe.wait_ge(acc_done, PAIRS)
            pe.wait_ge(h_ready, SHARED * PAIRS * FC)
            gather_transpose(0, 0, 0, True)
            expert = experts_of(0, NG)
            for k in range(NG):
                gather_transpose(k + 1, (k + 1) % NG, 0 if k < NG - 1 else 1, k == 0)
                routed_up(k, k, expert[k], k < 2)
                if k:
                    routed_down(k - 1, k - 1, expert[k - 1], k < 3)
            with pe.Fori(1, ROUNDS) as n:
                expert = experts_of(NG * n - 1, 2)
                for k in range(NG):
                    if k in (0, 2):
                        expert += experts_of(NG * n - 1 + len(expert), (3, 0, 4)[k])
                    gather_transpose(NG * n + k + 1, (k + 1) % NG, n if k < NG - 1 else n + 1)
                    routed_up(NG * n + k, k, expert[k + 1], False)
                    routed_down(NG * n + k - 1, (k - 1) % NG, expert[k], False)
            expert = experts_of(NG * ROUNDS - 1, REST + 1)
            for k in range(REST):
                i = NG * ROUNDS + k
                if k < REST - 1:
                    gather_transpose(i + 1, k + 1, ROUNDS)
                routed_up(i, k, expert[k + 1], False)
                routed_down(i - 1, (k - 1) % NG, expert[k], False)
            routed_down(MAX_TILES - 1, REST - 1, expert[REST], False)


def kernel(**inputs):
    import concourse.bacc as bacc
    from concourse.bass_utils import run_bass_kernel_spmd

    f32 = {k: np.asarray(v) for k, v in inputs.items()}
    arrays = {
        "x": f32["x"].reshape(B * S, D),
        "ctx_t": f32["ctx_1024"].reshape(PAIRS, 2, SK, D).transpose(3, 0, 1, 2),
        "wq_t": f32["L0_xattn_Wq"].T,
        "wk_t": f32["L0_xattn_Wk"].T,
        "wv_t": f32["L0_xattn_Wv"].T,
        "wo_t": f32["L0_xattn_Wo"].T,
        "cent_t": f32["L0_ffn_centroids"].T,
        "rbias": np.broadcast_to(f32["L0_ffn_routing_bias"], (P, EXPERTS)),
        "wfc_t": np.concatenate([f32["L0_ffn_Wfc_sh"], f32["L0_ffn_Wfc_r"]]).transpose(2, 0, 1),
        "wproj_t": np.concatenate([f32["L0_ffn_Wproj_sh"], f32["L0_ffn_Wproj_r"]])
                     .reshape(NE, D, FC, P).transpose(3, 0, 2, 1).reshape(P, NE, FC * D),
    }
    nc = bacc.Bacc("TRN2", target_bir_lowering=False, num_devices=1)
    arrays = {f"in_{k}": np.ascontiguousarray(a) for k, a in arrays.items()}
    aps = [nc.dram_tensor(k, a.shape, mybir.dt.from_np(a.dtype), kind="ExternalInput").ap()
           for k, a in arrays.items()]
    out = nc.dram_tensor("out", (B * S, D), F32, kind="ExternalOutput").ap()
    gathered = nc.dram_tensor("gathered", (EXPERTS * REGION + GT, ROW), F16, kind="Internal").ap()
    results = nc.dram_tensor("results", (2 * B * S, D), F32, kind="Internal").ap()
    xattn_moe_kernel(nc, *aps, out, gathered, results)
    r = run_bass_kernel_spmd(nc, [arrays], core_ids=[0])
    return r.results[0]["out"].reshape(B, S, D)
```
